# Optimizing a Trainium2 kernel written in Bass

```python
import numpy as np
import jax
import jax.numpy as jnp

def _softmax(x, axis=-1):
    return jax.nn.softmax(x, axis=axis)

def _gelu(x):
    return jax.nn.gelu(x, approximate=True)

def _silu(x):
    return jax.nn.silu(x)

def _sigmoid(x):
    return jax.nn.sigmoid(x)

def _layernorm(x, axis=-1, eps=1e-05):
    m = jnp.mean(x, axis=axis, keepdims=True)
    v = jnp.var(x, axis=axis, keepdims=True)
    return (x - m) / jnp.sqrt(v + eps)

def _scatter_add(tgt, idx, src, axis=0):
    return tgt.at[idx].add(src)

def _segment_sum(src, seg, n):
    return jax.ops.segment_sum(src, seg, n)
kernel_name = 'mk_gnn_preln_d2_gnn_r8_c0dd5c'

def setup_inputs(seed: int=0):
    np.random.seed(seed)
    _w = jnp.asarray

    def _rec_inputs():
        import jax
        import jax.numpy as jnp
        _gk = jax.random.key(seed)
        x = -0.0001006 + 1 * jax.random.normal(jax.random.fold_in(_gk, 1), (12500, 96), jnp.float32)
        src = jax.random.randint(jax.random.fold_in(_gk, 2), (400000,), 0, 12500, jnp.int32)
        dst = jax.random.randint(jax.random.fold_in(_gk, 3), (400000,), 0, 12500, jnp.int32)
        _o = jnp.argsort(dst, stable=True)
        src = src[_o]
        dst = dst[_o]
        edge_attr_32 = 0.000196303 + 1.00016 * jax.random.normal(jax.random.fold_in(_gk, 12), (400000, 32), jnp.float32)
        return (x, src, dst, edge_attr_32)
    x, src, dst, edge_attr_32 = _rec_inputs()

    def _L0_gnn_setup():
        import jax, jax.numpy as jnp
        import numpy as np
        N_NODES = 6250
        N_EDGES = 100000
        D = 96
        DEPTH = 2
        key = jax.random.key(seed)
        ks = jax.random.split(key, 8)
        scale = 1.0 / np.sqrt(D)
        x = jax.random.normal(ks[0], (N_NODES, D), dtype=jnp.float32)
        W0 = jax.random.normal(ks[1], (DEPTH, D, D), dtype=jnp.float32) * scale
        b0 = jnp.zeros((DEPTH, D), dtype=jnp.float32)
        W1 = jax.random.normal(ks[2], (DEPTH, D, D), dtype=jnp.float32) * scale
        b1 = jnp.zeros((DEPTH, D), dtype=jnp.float32)
        W2 = jax.random.normal(ks[3], (DEPTH, 2 * D, D), dtype=jnp.float32) * (1.0 / np.sqrt(2 * D))
        b2 = jnp.zeros((DEPTH, D), dtype=jnp.float32)
        edge_src = jax.random.randint(ks[4], (N_EDGES,), 0, N_NODES, dtype=jnp.int64 if jax.config.jax_enable_x64 else jnp.int32)
        edge_dst = jnp.sort(jax.random.randint(ks[5], (N_EDGES,), 0, N_NODES, dtype=jnp.int64 if jax.config.jax_enable_x64 else jnp.int32))
        return {'x': x, 'W0': W0, 'b0': b0, 'W1': W1, 'b1': b1, 'W2': W2, 'b2': b2, 'edge_src': edge_src, 'edge_dst': edge_dst}
    _L0_gnn_all = _L0_gnn_setup()
    _L0_gnn_in = {k: v for k, v in _L0_gnn_all.items() if k in ('W0', 'b0', 'W1', 'b1', 'W2', 'b2')}
    del _L0_gnn_all

    def _L1_gnn_setup():
        import jax, jax.numpy as jnp
        import numpy as np
        N, E = (6250, 100000)
        ND, ED = (96, 32)

        def _gelu(x):
            return jax.nn.gelu(x, approximate=False)
        key = jax.random.key(seed)
        ks = jax.random.split(key, 16)
        s = lambda fan_in: 1.0 / np.sqrt(fan_in)
        inp = {'x': jax.random.normal(ks[0], (N, ND), jnp.float32), 'edge_index': jax.random.randint(ks[1], (2, E), 0, N, jnp.int32), 'edge_attr': jax.random.normal(ks[2], (E, ED), jnp.float32), 'mW1': jax.random.uniform(ks[3], (ND + ED, ND), jnp.float32, -s(ND + ED), s(ND + ED)), 'mb1': jnp.zeros((ND,), jnp.float32), 'mW2': jax.random.uniform(ks[4], (ND, ND), jnp.float32, -s(ND), s(ND)), 'mb2': jnp.zeros((ND,), jnp.float32), 'gW1': jax.random.uniform(ks[5], (ND + ED, ND), jnp.float32, -s(ND + ED), s(ND + ED)), 'gb1': jnp.zeros((ND,), jnp.float32), 'gW2': jax.random.uniform(ks[6], (ND, 1), jnp.float32, -s(ND), s(ND)), 'gb2': jnp.zeros((1,), jnp.float32), 'uW1': jax.random.uniform(ks[7], (2 * ND, ND), jnp.float32, -s(2 * ND), s(2 * ND)), 'ub1': jnp.zeros((ND,), jnp.float32), 'uW2': jax.random.uniform(ks[8], (ND, ND), jnp.float32, -s(ND), s(ND)), 'ub2': jnp.zeros((ND,), jnp.float32), 'ln_g': jnp.ones((ND,), jnp.float32), 'ln_b': jnp.zeros((ND,), jnp.float32)}
        return inp
    _L1_gnn_all = _L1_gnn_setup()
    _L1_gnn_in = {k: v for k, v in _L1_gnn_all.items() if k in ('mW1', 'mb1', 'mW2', 'mb2', 'gW1', 'gb1', 'gW2', 'gb2', 'uW1', 'ub1', 'uW2', 'ub2', 'ln_g', 'ln_b')}
    del _L1_gnn_all
    return {'x': x, 'src': src, 'dst': dst, 'edge_attr_32': edge_attr_32, 'L0_gnn_W0': _L0_gnn_in['W0'], 'L0_gnn_b0': _L0_gnn_in['b0'], 'L0_gnn_W1': _L0_gnn_in['W1'], 'L0_gnn_b1': _L0_gnn_in['b1'], 'L0_gnn_W2': _L0_gnn_in['W2'], 'L0_gnn_b2': _L0_gnn_in['b2'], 'L1_gnn_mW1': _L1_gnn_in['mW1'], 'L1_gnn_mb1': _L1_gnn_in['mb1'], 'L1_gnn_mW2': _L1_gnn_in['mW2'], 'L1_gnn_mb2': _L1_gnn_in['mb2'], 'L1_gnn_gW1': _L1_gnn_in['gW1'], 'L1_gnn_gb1': _L1_gnn_in['gb1'], 'L1_gnn_gW2': _L1_gnn_in['gW2'], 'L1_gnn_gb2': _L1_gnn_in['gb2'], 'L1_gnn_uW1': _L1_gnn_in['uW1'], 'L1_gnn_ub1': _L1_gnn_in['ub1'], 'L1_gnn_uW2': _L1_gnn_in['uW2'], 'L1_gnn_ub2': _L1_gnn_in['ub2'], 'L1_gnn_ln_g': _L1_gnn_in['ln_g'], 'L1_gnn_ln_b': _L1_gnn_in['ln_b']}

def reference(x, src, dst, edge_attr_32, L0_gnn_W0, L0_gnn_b0, L0_gnn_W1, L0_gnn_b1, L0_gnn_W2, L0_gnn_b2, L1_gnn_mW1, L1_gnn_mb1, L1_gnn_mW2, L1_gnn_mb2, L1_gnn_gW1, L1_gnn_gb1, L1_gnn_gW2, L1_gnn_gb2, L1_gnn_uW1, L1_gnn_ub1, L1_gnn_uW2, L1_gnn_ub2, L1_gnn_ln_g, L1_gnn_ln_b):
    import jax
    import jax.numpy as jnp

    def _L0_gnn_ref(x, W0, b0, W1, b1, W2, b2, edge_src, edge_dst):
        import jax, jax.numpy as jnp
        import numpy as np
        N_NODES = 6250
        N_EDGES = 100000
        D = 96
        DEPTH = 2
        n = x.shape[0]
        depth = W0.shape[0]
        for i in range(depth):
            h_self = x @ W1[i] + b1[i]
            h_nb = x @ W0[i] + b0[i]
            agg = jax.ops.segment_sum(h_nb[edge_src], edge_dst, num_segments=n)
            x = jnp.concatenate([h_self, agg], axis=-1) @ W2[i] + b2[i]
            x = x / jnp.std(x, axis=-1, ddof=1, keepdims=True)
        return x

    def _L1_gnn_ref(x, edge_index, edge_attr, mW1, mb1, mW2, mb2, gW1, gb1, gW2, gb2, uW1, ub1, uW2, ub2, ln_g, ln_b):
        import jax, jax.numpy as jnp
        import numpy as np
        N, E = (6250, 100000)
        ND, ED = (96, 32)

        def _gelu(x):
            return jax.nn.gelu(x, approximate=False)
        src, dst = (edge_index[0], edge_index[1])
        edge_input = jnp.concatenate([x[src], edge_attr], axis=-1)
        messages = _gelu(edge_input @ mW1 + mb1) @ mW2 + mb2
        gates = jax.nn.sigmoid(_gelu(edge_input @ gW1 + gb1) @ gW2 + gb2)
        aggregated = jax.ops.segment_sum(messages * gates, dst, num_segments=x.shape[0])
        combined = jnp.concatenate([x, aggregated], axis=-1)
        update = _gelu(combined @ uW1 + ub1) @ uW2 + ub2
        h = x + update
        mu = jnp.mean(h, axis=-1, keepdims=True)
        var = jnp.mean(jnp.square(h - mu), axis=-1, keepdims=True)
        return (h - mu) * jax.lax.rsqrt(var + 1e-05) * ln_g + ln_b
    edge_index = jnp.stack([src, dst])
    h = jnp.maximum(_layernorm(x, axis=-1), 0.0)
    x = x + _L0_gnn_ref(h, L0_gnn_W0, L0_gnn_b0, L0_gnn_W1, L0_gnn_b1, L0_gnn_W2, L0_gnn_b2, src, dst)
    h = jnp.maximum(_layernorm(x, axis=-1), 0.0)
    x = x + _L1_gnn_ref(h, edge_index, edge_attr_32, L1_gnn_mW1, L1_gnn_mb1, L1_gnn_mW2, L1_gnn_mb2, L1_gnn_gW1, L1_gnn_gb1, L1_gnn_gW2, L1_gnn_gb2, L1_gnn_uW1, L1_gnn_ub1, L1_gnn_uW2, L1_gnn_ub2, L1_gnn_ln_g, L1_gnn_ln_b)
    return x

_drawn_inputs = setup_inputs


def setup_inputs(seed=0):
    import zlib

    import numpy as np

    out = dict(_drawn_inputs(seed))
    spreads = {'L0_gnn_b0': (0.0, 0.1),
     'L0_gnn_b1': (0.0, 0.8),
     'L0_gnn_b2': (0.0, 0.8),
     'L1_gnn_mb1': (0.0, 0.1),
     'L1_gnn_mb2': (0.0, 0.1),
     'L1_gnn_gb1': (0.0, 2.0),
     'L1_gnn_ub1': (0.0, 0.291),
     'L1_gnn_ub2': (0.0, 0.1),
     'L1_gnn_ln_g': (1.0, 0.2),
     'L1_gnn_ln_b': (0.0, 0.1)}
    factors = {'L1_gnn_gW1': 8.0, 'L1_gnn_gW2': 8.0}
    for name, (base, spread) in spreads.items():
        noise = np.random.default_rng([zlib.crc32(name.encode()), seed]).standard_normal(out[name].shape)
        drawn = base * np.exp(spread * noise) if base else spread * noise
        out[name] = jnp.asarray(drawn.astype(out[name].dtype))
    for name, factor in factors.items():
        out[name] = (out[name] * factor).astype(out[name].dtype)
    return out
```

```python
import concourse.bass as bass
from concourse import mybir
from contextlib import ExitStack

F32 = mybir.dt.float32
I32 = mybir.dt.int32
ALU = mybir.AluOpType
ACT = mybir.ActivationFunctionType
AX = mybir.AxisListType

N, E, D, ED = 12500, 400000, 96, 32
D1 = D + 1
P = 128
EPS = 1e-5

UNROLL = 5
TILES = 5
CE = TILES * P
CHUNKS = E // CE
BODIES = CHUNKS // UNROLL
WIN_BITS = 6
WIN = 1 << WIN_BITS
ROUNDS_MAX = (N - 1) // WIN + 1

NB = 100
BL = 5
GN = NB * BL
GROUPS = N // GN
GBODIES = GROUPS // UNROLL
assert CHUNKS * CE == E and BODIES * UNROLL == CHUNKS and GBODIES * UNROLL * GN == N

RING5, BACK5 = [0, 1, 2, 3, 4], [5, 5, 5, 5, 5]
RING2, BACK2 = [0, 1, 0, 1, 0], [1, 3, 2, 2, 2]
RING1, BACK1 = [0] * 5, [1] * 5
CREDIT = 5


def free_at(count, back):
    return count + (CREDIT + 1 - back)


def done_at(count):
    return count + (CREDIT + 1)


def skewed(eng, bodies, before, stages):

    def emit(first, k, skew, stage):
        back = 1 if k < skew else 0
        body = first - back if back else first
        kk = k - skew + UNROLL * back
        total = body + before if before is not None else body
        stage(body * UNROLL + kk, kk, total * UNROLL + kk, total)

    for k in range(UNROLL):
        for stage, skew in stages:
            if k >= skew:
                emit(0, k, skew, stage)
    with eng.Fori(1, bodies) as b:
        for k in range(UNROLL):
            for stage, skew in stages:
                emit(b, k, skew, stage)
    for k in range(max(skew for _, skew in stages)):
        for stage, skew in stages:
            if k < skew:
                emit(bodies, k, skew, stage)


def gnn(nc, x, src, dst_tiles, dst_rows, edge_t, W0T, b0, W1T, b1, W2, b2, mW1, mb1, mW2T, mb2,
        gW1, gb1, gW2, gb2, uW1, ub1, uW2, ub2, ln_g, ln_b, out,
        rows_h, rows_x1, rows_p, x_mid, extents):
    ctx = ExitStack()
    with ctx:
        def sb(name, shape, dt=F32):
            return ctx.enter_context(nc.sbuf_tensor(name, shape, dt))

        feat = sb("feat", [D1, N])
        sums = sb("sums", [P, N + WIN])
        dst_rel = sb("dst_rel", [P, CHUNKS * TILES])
        start0 = sb("start0", [1, CHUNKS])
        start_f = sb("start_f", [1, CHUNKS])
        start_i = sb("start_i", [1, CHUNKS], I32)
        rounds_i = sb("rounds_i", [P, 1], I32)
        rounds_w = sb("rounds_w", [P, 1])
        ident = sb("ident", [P, P])
        window = sb("window", [P, WIN])
        wa = sb("wa", [D1, 2, D])
        wb = sb("wb", [D1, 2, D])
        w_pre = sb("w_pre", [D1, 2 * D])
        w_edge = sb("w_edge", [ED, 2 * D])
        wu_self = sb("wu_self", [D1, D])
        wu_sum = sb("wu_sum", [D1, D])
        uw2 = sb("uw2", [D, D])
        ub2_col = sb("ub2_col", [D, 1])
        gw2_row = sb("gw2_row", [P, D])
        gb2_half = sb("gb2_half", [P, 1])
        lng_row = sb("lng_row", [NB, D])
        lnb_row = sb("lnb_row", [NB, D])
        eps_col = sb("eps_col", [NB, 1])
        idx = sb("idx", [P, 5, TILES], I32)
        got = sb("got", [P, 5, TILES * 2 * D])
        hot = sb("hot", [P, 5, TILES, WIN])
        msg = sb("msg", [P, 5, TILES, D1])
        edge_room = sb("edge_room", [P, 5, CE])
        edge = edge_room[0:ED, :, :]
        zz = sb("zz", [P, 5, TILES])
        gate = sb("gate", [P, 5, TILES])
        spare = edge_room[0:NB, :, 0:BL * D].rearrange("p k (b f) -> p k b f", f=D)
        xin = sb("xin", [NB, 5, BL, D])
        row = sb("row", [NB, 5, BL, D])

        def semaphores(own):
            used = []

            def name(n):
                used.append(nc.alloc_semaphore(name=n))
                return used[-1]

            def clear():
                nc.clear_and_free_semaphores(used)
                nc.all_engine_barrier()

            own.callback(clear)
            return (lambda *list_: [name(n) for n in list_]), (lambda n: [name(f"{n}{k}") for k in range(5)])

        passed = ctx.enter_context(nc.semaphore("passed"))

        def hold(eng):
            eng.sem_inc(passed, 1)

        with ExitStack() as own:
            names, slots = semaphores(own)

            def ps(name, shape):
                return own.enter_context(nc.psum_tensor(name, shape, F32))

            def tmp(name, shape, dt=F32):
                return own.enter_context(nc.sbuf_tensor(name, shape, dt))

            w0t = tmp("w0t", [D, 2, D1])
            w1t = tmp("w1t", [D, 2, D1])
            mw2t = tmp("mw2t", [D, D1])
            w2a = tmp("w2a", [D, 2, D])
            w2b = tmp("w2b", [D, 2, D])
            uw1b = tmp("uw1b", [D, D])
            b2r = tmp("b2r", [1, 2, D])
            last_row = tmp("last_row", [1, D1])
            lo = tmp("lo", [BODIES, UNROLL])
            hi = tmp("hi", [BODIES, UNROLL])
            starts = tmp("starts", [P, CHUNKS])
            widest = tmp("widest", [P, 4])
            widest_i = tmp("widest_i", [P, 2], I32)
            p_w = ps("p_w", [D1, 5, 512])
            dst_i = got[:, :, :].rearrange("p a b -> p (a b)")[:, 0:CHUNKS * TILES].bitcast(I32)
            dst_c = sums[0:BODIES, 0:UNROLL * CE].bitcast(I32).rearrange("p (u e) -> p u e", u=UNROLL)
            (w_in, dst_in, tiles_in, iota_done, sel_set, w_mul, w_out, lohi, ext_out, ext_in, wide,
             consts) = names("w_in", "dst_in", "tiles_in", "iota_done", "sel_set", "w_mul", "w_out",
                             "lohi", "ext_out", "ext_in", "wide", "consts")
            block = own.enter_context(nc.Block())

            @block.sync
            def _(sp):
                sp.dma_start(dst_c, dst_rows).then_inc(dst_in, 16)
                sp.dma_start(dst_i, dst_tiles).then_inc(tiles_in, 16)
                sp.wait_ge(lohi, 2)
                sp.dma_start(extents[0], lo[:, :]).then_inc(ext_out, 16)
                sp.dma_start(extents[1], hi[:, :]).then_inc(ext_out, 16)
                sp.wait_ge(ext_out, 32)
                flat = extents.rearrange("a b u -> a (b u)")
                sp.dma_start(starts[:, :], flat[0:1, :].partition_broadcast(P)).then_inc(ext_in, 16)
                sp.dma_start(hot[:, 0:2, :, :].rearrange("p a b c -> p (a b c)")[:, 0:CHUNKS],
                             flat[1:2, :].partition_broadcast(P)).then_inc(ext_in, 16)

            @block.scalar
            def _(act):
                loads = [(w_pre[0:D, 0:D], mW1[0:D, :]), (w_pre[0:D, D:2 * D], gW1[0:D, :]),
                         (w_pre[D:D1, 0:D], mb1), (w_pre[D:D1, D:2 * D], gb1),
                         (w_edge[:, 0:D], mW1[D:D + ED, :]), (w_edge[:, D:2 * D], gW1[D:D + ED, :]),
                         (wu_self[0:D, :], uW1[0:D, :]), (wu_self[D:D1, :], ub1),
                         (uw1b[:, :], uW1[D:2 * D, :]), (uw2[:, :], uW2), (ub2_col[:, :], ub2),
                         (gw2_row[:, :], gW2.partition_broadcast(P)),
                         (gb2_half[:, :], gb2.partition_broadcast(P)),
                         (lng_row[:, :], ln_g.partition_broadcast(NB)),
                         (lnb_row[:, :], ln_b.partition_broadcast(NB)),
                         (mw2t[:, 0:D], mW2T), (mw2t[:, D:D1], mb2)]
                for i in range(2):
                    loads += [(w0t[:, i, 0:D], W0T[i]), (w0t[:, i, D:D1], b0[i]),
                              (w1t[:, i, 0:D], W1T[i]), (w1t[:, i, D:D1], b1[i]),
                              (w2a[:, i, :], W2[i, 0:D, :]), (w2b[:, i, :], W2[i, D:2 * D, :]),
                              (b2r[:, i, :], b2[i])]
                for to, of in loads:
                    act.dma_start(to, of).then_inc(w_in, 16)
                act.wait_ge(w_in, 16 * len(loads))
                act.mul(gb2_half[:, :], gb2_half[:, :], 0.5).then_inc(w_out, 1)
                act.wait_ge(w_mul, 1)
                for n, to in enumerate((wa[:, 0, :], wa[:, 1, :], wb[:, 0, :], wb[:, 1, :], wu_sum[:, :])):
                    act.activation(to, p_w[:, n, 0:D], ACT.Copy).then_inc(w_out, 1)
                act.wait_ge(w_out, 6)

            @block.gpsimd
            def _(pool):
                pool.iota(starts[:, 0:WIN].bitcast(I32), pattern=[[1, WIN]], base=0,
                          channel_multiplier=0).then_inc(iota_done, 1)
                pool.memset(ident[:, :], 0.0).then_inc(sel_set, 1)
                pool.wait_ge(sel_set, 1)
                pool.affine_select(out=ident[:, :], in_=ident[:, :], compare_op=ALU.not_equal,
                                   fill=1.0, base=0, pattern=[[-1, P]], channel_multiplier=1)\
                    .then_inc(sel_set, 1)
                pool.wait_ge(sel_set, 2)

            @block.vector
            def _(dve):
                dve.memset(last_row[:, :], 0.0).then_inc(consts, 1)
                dve.memset(feat[D:D1, :], 1.0).then_inc(consts, 1)
                dve.memset(msg[:, :, :, D:D1], 1.0).then_inc(consts, 1)
                dve.memset(eps_col[:, :], EPS).then_inc(consts, 1)
                dve.wait_ge(consts, 4)
                dve.memset(last_row[:, D:D1], 1.0).then_inc(consts, 1)
                dve.wait_ge(iota_done, 1)
                dve.tensor_copy(window[:, :], starts[:, 0:WIN].bitcast(I32)).then_inc(iota_done, 1)
                dve.wait_ge(dst_in, 16)
                dve.tensor_reduce(lo[:, :], dst_c, AX.X, ALU.min).then_inc(lohi, 1)
                dve.tensor_reduce(hi[:, :], dst_c, AX.X, ALU.max).then_inc(lohi, 1)
                dve.wait_ge(iota_done, 2)
                dve.wait_ge(ext_in, 32)
                his = hot[:, 0:2, :, :].rearrange("p a b c -> p (a b c)")[:, 0:CHUNKS]
                dve.tensor_tensor(his, his, starts[:, :], ALU.subtract).then_inc(wide, 1)
                dve.tensor_copy(start0[:, :], starts[0:1, :]).then_inc(wide, 1)
                dve.tensor_copy(start_f[:, :], starts[0:1, :]).then_inc(wide, 1)
                dve.tensor_copy(start_i[:, :], starts[0:1, :]).then_inc(wide, 1)
                dve.wait_ge(wide, 4)
                dve.tensor_reduce(widest[:, 0:1], his, AX.X, ALU.max).then_inc(wide, 1)
                dve.wait_ge(wide, 5)
                dve.tensor_copy(widest_i[:, 0:1], widest[:, 0:1]).then_inc(wide, 1)
                dve.wait_ge(wide, 6)
                dve.tensor_scalar(widest_i[:, 1:2], widest_i[:, 0:1], WIN_BITS, None,
                                  ALU.arith_shift_right).then_inc(wide, 1)
                dve.wait_ge(wide, 7)
                dve.tensor_scalar(widest[:, 1:2], widest_i[:, 1:2], 1.0, None, ALU.add).then_inc(wide, 1)
                dve.wait_ge(wide, 8)
                dve.tensor_copy(rounds_i[:, :], widest[:, 1:2]).then_inc(wide, 1)
                dve.tensor_scalar(rounds_w[:, :], widest[:, 1:2], float(WIN), None, ALU.mult)\
                    .then_inc(wide, 1)
                dve.wait_ge(tiles_in, 16)
                dve.tensor_tensor(dst_rel[:, :].rearrange("p (c t) -> p c t", t=TILES),
                                  dst_i.rearrange("p (c t) -> p c t", t=TILES),
                                  starts[:, :].unsqueeze(2).broadcast_to([P, CHUNKS, TILES]),
                                  ALU.subtract).then_inc(wide, 1)
                dve.wait_ge(wide, 11)

            @block.tensor
            def _(pe):
                pe.wait_ge(w_in, 16 * 31)
                pe.wait_ge(consts, 5)
                for i in range(2):
                    pe.matmul(p_w[:, i, 0:D], w1t[:, i, :], w2a[:, i, :], start=True, stop=False)
                    pe.matmul(p_w[:, i, 0:D], last_row[:, :], b2r[:, i, :], start=False, stop=True)
                    pe.matmul(p_w[:, 2 + i, 0:D], w0t[:, i, :], w2b[:, i, :], start=True, stop=True)
                pe.matmul(p_w[:, 4, 0:D], mw2t[:, :], uw1b[:, :], start=True, stop=True).then_inc(w_mul, 1)

        def node_rows(table, g):
            return table[bass.ds(g * GN, GN), :].rearrange("(b p) f -> p b f", p=NB)

        def columns(t, rows, g):
            return t[0:rows, bass.ds(g * GN, GN)]

        def over(col, width=D):
            return col.unsqueeze(2).broadcast_to([NB, BL, width])

        def node_norm_first():
            with ExitStack() as own:
                names, slots = semaphores(own)

                def tmp(name, shape):
                    return own.enter_context(nc.sbuf_tensor(name, shape, F32))

                stat = tmp("n0_stat", [NB, 5, BL, 6])
                mean_var = tmp("n0_mv", [NB, 5, BL, 2])
                std = tmp("n0_std", [NB, 5, BL])
                cent = spare
                p_t = own.enter_context(nc.psum_tensor("n0_pt", [D, 2, 512], F32))
                x_ready, row_stored = slots("n0_x_ready"), slots("n0_stored")
                (stat_done, var_done, std_done, rstd_done, cent_done, norm_done, row_done, turned,
                 row_free, feat_done) = names("n0_stat_done", "n0_var_done", "n0_std_done",
                                              "n0_rstd_done", "n0_cent_done", "n0_norm_done",
                                              "n0_row_done", "n0_turned", "n0_row_free",
                                              "n0_feat_done")
                block = own.enter_context(nc.Block())

                @block.sync
                def _(sp):
                    sp.sem_inc(row_free, CREDIT)

                    def load(g, k, count, body):
                        sp.wait_ge(cent_done, free_at(count, BACK5[k]))
                        sp.dma_start(xin[:, k, :, :], node_rows(x, g)).then_inc(x_ready[k], 16)

                    def store(g, k, count, body):
                        sp.wait_ge(row_done, done_at(count))
                        sp.dma_start(node_rows(rows_h, g), row[:, k, :, :]).then_inc(row_stored[k], 16)

                    def stored(g, k, count, body):
                        sp.wait_ge(row_stored[k], 16 * (body + 1))
                        sp.sem_inc(row_free, 1)

                    skewed(sp, GBODIES, None, [(load, 0), (store, 3), (stored, 4)])

                @block.vector
                def _(dve):
                    dve.sem_inc(cent_done, CREDIT)

                    def statistics(g, k, count, body):
                        dve.wait_ge(x_ready[k], 16 * (body + 1))
                        dve.wait_ge(std_done, free_at(count, BACK5[k]))
                        for b in range(BL):
                            dve.bn_stats(stat[:, k, b, :], xin[:, k, b, :]).then_inc(stat_done, 1)
                        dve.wait_ge(stat_done, count * BL + BL)
                        hold(dve)
                        for b in range(BL):
                            i = dve.bn_aggr(mean_var[:, k, b, :], stat[:, k, b, :])
                        i.then_inc(var_done, 1)

                    def centre(g, k, count, body):
                        dve.wait_ge(var_done, count + 1)
                        dve.wait_ge(row_done, free_at(count, BACK5[k]))
                        dve.tensor_tensor(cent[:, k, :, :], xin[:, k, :, :],
                                          over(mean_var[:, k, :, 0]), ALU.subtract)\
                            .then_inc(cent_done, 1)
                        dve.wait_ge(std_done, done_at(count))
                        dve.reciprocal(std[:, k, :], std[:, k, :]).then_inc(rstd_done, 1)
                        dve.wait_ge(rstd_done, count + 1)
                        dve.wait_ge(cent_done, done_at(count))
                        dve.tensor_tensor(cent[:, k, :, :], cent[:, k, :, :], over(std[:, k, :]),
                                          ALU.mult).then_inc(norm_done, 1)

                    skewed(dve, GBODIES, None, [(statistics, 0), (centre, 1)])

                @block.scalar
                def _(act):
                    act.sem_inc(std_done, CREDIT)
                    act.sem_inc(row_done, CREDIT)
                    act.sem_inc(feat_done, CREDIT)

                    def root(g, k, count, body):
                        act.wait_ge(var_done, count + 1)
                        act.activation(std[:, k, :], mean_var[:, k, :, 1], ACT.Sqrt,
                                       bias=eps_col[:, :]).then_inc(std_done, 1)

                    def relu(g, k, count, body):
                        act.wait_ge(norm_done, count + 1)
                        act.wait_ge(row_free, free_at(count, BACK5[k]))
                        act.activation(row[:, k, :, :], cent[:, k, :, :], ACT.Relu).then_inc(row_done, 1)

                    def keep(g, k, count, body):
                        act.wait_ge(turned, count + 1)
                        act.activation(columns(feat, D, g), p_t[:, RING2[k], 0:GN], ACT.Copy)\
                            .then_inc(feat_done, 1)

                    skewed(act, GBODIES, None, [(root, 0), (relu, 1), (keep, 2)])

                @block.tensor
                def _(pe):
                    def turn(g, k, count, body):
                        pe.wait_ge(row_done, done_at(count))
                        pe.wait_ge(feat_done, free_at(count, BACK2[k]))
                        for b in range(BL):
                            i = pe.transpose(p_t[:, RING2[k], b * NB:(b + 1) * NB], row[:, k, b, :],
                                             ident[0:NB, 0:NB])
                        i.then_inc(turned, 1)

                    skewed(pe, GBODIES, None, [(turn, 0)])


        def load_indices(sp, name, idx_ready, gathered, more=None):
            rounds = sp.value_load(rounds_i[0:1, 0:1], min_val=1, max_val=ROUNDS_MAX)
            for k in range(UNROLL):
                sp.dma_start(idx[:, k, :], src[k]).then_inc(idx_ready[k], 16)
                if more:
                    more(k, k, None)
            with sp.Fori(0, rounds) as r:
                with sp.Fori(1, BODIES) as b:
                    for k in range(UNROLL):
                        sp.wait_ge(gathered[k], (r * BODIES + b) * (16 * TILES))
                        sp.dma_start(idx[:, k, :], src[bass.ds(b * UNROLL + k, 1)].rearrange(
                            "c p t -> (c p) t")).then_inc(idx_ready[k], 16)
                        if more:
                            more(b * UNROLL + k, k, (r * BODIES + b) * UNROLL + k)
                for k in range(UNROLL):
                    sp.wait_ge(gathered[k], (r * BODIES + BODIES) * (16 * TILES))
                    sp.dma_start(idx[:, k, :], src[k]).then_inc(idx_ready[k], 16)
                    if more:
                        more(k, k, (r * BODIES + BODIES) * UNROLL + k)
            for k in range(UNROLL):
                sp.wait_ge(idx_ready[k], rounds * (16 * BODIES) + 16)
                hold(sp)


        def gather_rows(pool, table, width, pitch, idx_ready, gathered, free):
            rounds = pool.value_load(rounds_i[0:1, 0:1], min_val=1, max_val=ROUNDS_MAX)
            with pool.Fori(0, rounds) as r:
                with pool.Fori(0, BODIES) as b:
                    for k in range(UNROLL):
                        body = r * BODIES + b
                        pool.wait_ge(idx_ready[k], body * 16 + 16)
                        hold(pool)
                        pool.wait_ge(free, body * UNROLL + (k + 1))
                        hold(pool)
                        for t in range(TILES):
                            pool.indirect_dma_start(
                                got[:, k, t * pitch:t * pitch + width], None, table,
                                bass.IndirectOffsetOnAxis(idx[:, k, t:t + 1], axis=0))\
                                .then_inc(gathered[k], 16)

        def one_hot(dve, chunk, k):
            rel = dst_rel[:, bass.ds(chunk * TILES, TILES)].unsqueeze(2).broadcast_to([P, TILES, WIN])
            cols = window[:, :].unsqueeze(1).broadcast_to([P, TILES, WIN])
            return dve.tensor_tensor(hot[:, k, :, :], rel, cols, ALU.is_equal)

        def add_window(dve, chunk, p_seg_slot, start_reg):
            dve.reg_load(start_reg, start_i[0:1, bass.ds(chunk, 1)])
            start = dve.snap(start_reg, min_val=0, max_val=N)
            where = sums[0:D1, bass.ds(start, WIN)]
            return dve.tensor_tensor(where, where, p_seg_slot, ALU.add)

        def move_windows(dve, moved, r):
            dve.tensor_scalar(dst_rel[:, :], dst_rel[:, :], float(-WIN), None, ALU.add).then_inc(moved, 1)
            dve.tensor_scalar(start_f[:, :], start_f[:, :], float(WIN), None, ALU.add).then_inc(moved, 1)
            dve.wait_ge(moved, r * 3 + 2)
            dve.tensor_scalar(start_i[:, :], start_f[:, :], float(N), None, ALU.min).then_inc(moved, 1)
            dve.wait_ge(moved, r * 3 + 3)
            hold(dve)

        def restore_windows(dve, back):
            dve.tensor_scalar(dst_rel[:, :], dst_rel[:, :], rounds_w[:, 0:1], None, ALU.add).then_inc(back, 1)
            dve.tensor_copy(start_f[:, :], start0[:, :]).then_inc(back, 1)
            dve.tensor_copy(start_i[:, :], start0[:, :]).then_inc(back, 1)
            dve.wait_ge(back, 3)

        def linear_pass(name, table):
            with ExitStack() as own:
                names, slots = semaphores(own)
                p_seg = own.enter_context(nc.psum_tensor(name + "_seg", [D1, 5, 512], F32))
                idx_ready, gathered = slots(name + "_idx_ready"), slots(name + "_gathered")
                hot_done, seg_done, added, zeroed, moved, back = names(
                    name + "_hot_done", name + "_seg_done", name + "_added", name + "_zeroed",
                    name + "_moved", name + "_back")
                block = own.enter_context(nc.Block())

                def rows_of(k):
                    return got[:, k, 0:TILES * D1].rearrange("p (t f) -> p t f", f=D1)

                @block.sync
                def _(sp):
                    load_indices(sp, name, idx_ready, gathered)

                @block.gpsimd
                def _(pool):
                    gather_rows(pool, table, D, D1, idx_ready, gathered, seg_done)

                @block.tensor
                def _(pe):
                    pe.sem_inc(seg_done, CREDIT)
                    rounds = pe.value_load(rounds_i[0:1, 0:1], min_val=1, max_val=ROUNDS_MAX)
                    pe.wait_ge(zeroed, 1)
                    hold(pe)
                    with pe.Fori(0, rounds) as r:
                        def segment(chunk, k, count, body):
                            pe.wait_ge(gathered[k], body * (16 * TILES) + 16 * TILES)
                            pe.wait_ge(hot_done, count + 1)
                            pe.wait_ge(added, free_at(count, BACK5[k]))
                            for t in range(TILES):
                                i = pe.matmul(p_seg[:, k, 0:WIN], rows_of(k)[:, t, :], hot[:, k, t, :],
                                              start=t == 0, stop=t == TILES - 1)
                            i.then_inc(seg_done, 1)

                        skewed(pe, BODIES, r * BODIES, [(segment, 0)])

                @block.vector
                def _(dve):
                    dve.sem_inc(added, CREDIT)
                    rounds = dve.value_load(rounds_i[0:1, 0:1], min_val=1, max_val=ROUNDS_MAX)
                    start_reg = dve.alloc_register(name + "_start")
                    for k in range(5):
                        i = dve.memset(rows_of(k)[:, :, D:D1], 1.0)
                    i.then_inc(zeroed, 1)
                    dve.memset(sums[:, :], 0.0).then_inc(zeroed, 1)
                    dve.wait_ge(zeroed, 2)
                    hold(dve)
                    with dve.Fori(0, rounds) as r:
                        def hots(chunk, k, count, body):
                            dve.wait_ge(seg_done, free_at(count, BACK5[k]))
                            one_hot(dve, chunk, k).then_inc(hot_done, 1)

                        def add(chunk, k, count, body):
                            dve.wait_ge(seg_done, done_at(count))
                            dve.wait_ge(added, free_at(count, 1))
                            hold(dve)
                            add_window(dve, chunk, p_seg[:, k, 0:WIN], start_reg).then_inc(added, 1)

                        skewed(dve, BODIES, r * BODIES, [(hots, 0), (add, 1)])
                        move_windows(dve, moved, r)
                    restore_windows(dve, back)
                    dve.wait_ge(added, rounds * CHUNKS + CREDIT)
                    hold(dve)

        def gated_pass(name, table):
            with ExitStack() as own:
                names, slots = semaphores(own)
                p_edge = own.enter_context(nc.psum_tensor(name + "_edge", [P, 2, 3, 512], F32))
                p_seg = own.enter_context(nc.psum_tensor(name + "_seg", [D1, 2, 512], F32))
                idx_ready, gathered = slots(name + "_idx_ready"), slots(name + "_gathered")
                edge_ready = slots(name + "_edge_ready")
                (edge_done, pre_done, msg_done, gelu_done, z_done, tanh_done, gate_done, eq_done,
                 hot_done, seg_done, added, zeroed, moved, back) = names(
                    *(name + "_" + n for n in ("edge_done", "pre_done", "msg_done", "gelu_done",
                                               "z_done", "tanh_done", "gate_done", "eq_done",
                                               "hot_done", "seg_done", "added", "zeroed", "moved",
                                               "back")))
                block = own.enter_context(nc.Block())

                def halves(k):
                    return got[:, k, :].rearrange("p (t h f) -> p t h f", h=2, f=D)

                @block.sync
                def _(sp):
                    def attributes(chunk, k, count):
                        if count is None:
                            of = edge_t[:, chunk * CE:(chunk + 1) * CE]
                        else:
                            sp.wait_ge(edge_done, count - (UNROLL - 1))
                            of = edge_t[:, bass.ds(chunk * CE, CE)]
                        sp.dma_start(edge[:, k, :], of).then_inc(edge_ready[k], 16)

                    load_indices(sp, name, idx_ready, gathered, attributes)
                    rounds = sp.value_load(rounds_i[0:1, 0:1], min_val=1, max_val=ROUNDS_MAX)
                    for k in range(UNROLL):
                        sp.wait_ge(edge_ready[k], rounds * (16 * BODIES) + 16)
                        hold(sp)

                @block.gpsimd
                def _(pool):
                    gather_rows(pool, table, 2 * D, 2 * D, idx_ready, gathered, z_done)

                @block.tensor
                def _(pe):
                    pe.sem_inc(seg_done, CREDIT)
                    rounds = pe.value_load(rounds_i[0:1, 0:1], min_val=1, max_val=ROUNDS_MAX)
                    with pe.Fori(0, rounds) as r:
                        def edges(chunk, k, count, body):
                            pe.wait_ge(edge_ready[k], body * 16 + 16)
                            pe.wait_ge(pre_done, free_at(count, BACK2[k]))
                            for t in range(TILES):
                                i = pe.matmul(p_edge[:, RING2[k], t // 2, t % 2 * 2 * D:(t % 2 + 1) * 2 * D],
                                              edge[:, k, t * P:(t + 1) * P], w_edge[:, :],
                                              start=True, stop=True)
                            i.then_inc(edge_done, 1)

                        def segment(chunk, k, count, body):
                            pe.wait_ge(msg_done, count + 1)
                            pe.wait_ge(hot_done, count + 1)
                            pe.wait_ge(added, free_at(count, BACK2[k]))
                            for t in range(TILES):
                                i = pe.matmul(p_seg[:, RING2[k], 0:WIN], msg[:, k, t, :], hot[:, k, t, :],
                                              start=t == 0, stop=t == TILES - 1)
                            i.then_inc(seg_done, 1)

                        skewed(pe, BODIES, r * BODIES, [(edges, 0), (segment, 3)])

                @block.scalar
                def _(act):
                    rounds = act.value_load(rounds_i[0:1, 0:1], min_val=1, max_val=ROUNDS_MAX)
                    with act.Fori(0, rounds) as r:
                        def gelus(chunk, k, count, body):
                            act.wait_ge(pre_done, done_at(count))
                            act.activation(halves(k)[:, :, 1, :], halves(k)[:, :, 1, :], ACT.Gelu)\
                                .then_inc(gelu_done, 1)
                            act.wait_ge(seg_done, free_at(count, BACK5[k]))
                            act.activation(msg[:, k, :, 0:D], halves(k)[:, :, 0, :], ACT.Gelu)\
                                .then_inc(msg_done, 1)

                        def tanh(chunk, k, count, body):
                            act.wait_ge(z_done, done_at(count))
                            act.activation(gate[:, k, :], zz[:, k, :], ACT.Tanh, scale=0.5,
                                           bias=gb2_half[:, :]).then_inc(tanh_done, 1)

                        skewed(act, BODIES, r * BODIES, [(gelus, 0), (tanh, 1)])

                @block.vector
                def _(dve):
                    dve.sem_inc(pre_done, CREDIT)
                    dve.sem_inc(z_done, CREDIT)
                    dve.sem_inc(added, CREDIT)
                    rounds = dve.value_load(rounds_i[0:1, 0:1], min_val=1, max_val=ROUNDS_MAX)
                    start_reg = dve.alloc_register(name + "_start")
                    dve.memset(sums[:, :], 0.0).then_inc(zeroed, 1)
                    dve.wait_ge(zeroed, 1)
                    hold(dve)
                    with dve.Fori(0, rounds) as r:
                        def pre(chunk, k, count, body):
                            dve.wait_ge(gathered[k], body * (16 * TILES) + 16 * TILES)
                            dve.wait_ge(edge_done, count + 1)
                            four = got[:, k, 0:8 * D].rearrange("p (b f) -> p b f", b=2)
                            dve.tensor_tensor(four, four, p_edge[:, RING2[k], 0:2, 0:4 * D], ALU.add)
                            one = got[:, k, 8 * D:10 * D]
                            dve.tensor_tensor(one, one, p_edge[:, RING2[k], 2, 0:2 * D], ALU.add)\
                                .then_inc(pre_done, 1)

                        def gate_sums(chunk, k, count, body):
                            dve.wait_ge(gelu_done, count + 1)
                            dve.wait_ge(msg_done, count + 1)
                            for t in range(TILES):
                                half = halves(k)[:, t, 1, :]
                                i = dve.tensor_tensor_reduce(out=half, in0=half, in1=gw2_row[:, :],
                                                             scale=1.0, scalar=0.0, op0=ALU.mult,
                                                             op1=ALU.add, accum_out=zz[:, k, t:t + 1])
                            i.then_inc(z_done, 1)

                        def gated_hots(chunk, k, count, body):
                            dve.wait_ge(seg_done, free_at(count, BACK5[k]))
                            one_hot(dve, chunk, k).then_inc(eq_done, 1)
                            dve.wait_ge(tanh_done, count + 1)
                            dve.tensor_scalar(gate[:, k, :], gate[:, k, :], 0.5, 0.5, ALU.mult,
                                              ALU.add).then_inc(gate_done, 1)
                            dve.wait_ge(eq_done, count + 1)
                            dve.wait_ge(gate_done, count + 1)
                            dve.tensor_tensor(hot[:, k, :, :], hot[:, k, :, :],
                                              gate[:, k, :].unsqueeze(2).broadcast_to([P, TILES, WIN]),
                                              ALU.mult).then_inc(hot_done, 1)

                        def add(chunk, k, count, body):
                            dve.wait_ge(seg_done, done_at(count))
                            dve.wait_ge(added, free_at(count, 1))
                            hold(dve)
                            add_window(dve, chunk, p_seg[:, RING2[k], 0:WIN], start_reg).then_inc(added, 1)

                        skewed(dve, BODIES, r * BODIES,
                               [(pre, 0), (gate_sums, 1), (gated_hots, 2), (add, 3)])
                        move_windows(dve, moved, r)
                    restore_windows(dve, back)
                    dve.wait_ge(added, rounds * CHUNKS + CREDIT)
                    hold(dve)

        def node_layer(name, layer, last):
            with ExitStack() as own:
                names, slots = semaphores(own)

                def tmp(n, shape):
                    return own.enter_context(nc.sbuf_tensor(name + n, shape, F32))

                def ps(n, shape):
                    return own.enter_context(nc.psum_tensor(name + n, shape, F32))

                stat = tmp("stat", [NB, 5, BL, 6])
                mean_var = tmp("mv", [NB, 5, BL, 2])
                std = tmp("std", [NB, 5, BL])
                y_t = tmp("y_t", [D, 2, GN])
                turned_s = tmp("turned_s", [D1, 2, GN])
                ring_p, back_p = (RING1, BACK1) if last else (RING2, BACK2)
                p_proj = ps("p_proj", [D, max(ring_p) + 1, 512])
                p_y = ps("p_y", [NB, 2, 512])
                p_turn = ps("p_turn", [D, 2, 512])
                if last:
                    stat2 = tmp("stat2", [NB, 5, BL, 6])
                    mean_var2 = tmp("mv2", [NB, 5, BL, 2])
                    std2 = tmp("std2", [NB, 5, BL])
                    mid = edge_room[0:NB, :, 0:BL * D].rearrange("p k (b f) -> p k b f", f=D)
                    p_pre = ps("p_pre", [NB, 3, 512])
                x_ready, row_stored = slots(name + "x_ready"), slots(name + "stored")
                mid_stored = slots(name + "mid_stored")
                (proj_done, y_t_done, y_done, stat_done, var_done, std_done, rstd_done, row_done,
                 row_free, turned, feat_done) = names(
                    *(name + n for n in ("proj_done", "y_t_done", "y_done", "stat_done", "var_done",
                                         "std_done", "rstd_done", "row_done", "row_free", "turned",
                                         "feat_done")))
                (scaled, mid_done, mid_free, stat2_done, var2_done, std2_done, rstd2_done, cent_done,
                 norm_done, turned_kept, pre_done, pre_kept, ones_set) = names(
                    *(name + n for n in ("scaled", "mid_done", "mid_free", "stat2_done", "var2_done",
                                         "std2_done", "rstd2_done", "cent_done", "norm_done",
                                         "turned_kept", "pre_done", "pre_kept", "ones_set")))
                y_used = scaled if last else row_done
                block = own.enter_context(nc.Block())

                def pre_rows(k):
                    return got[0:NB, k, :].rearrange("p (b f) -> p b f", f=2 * D)

                @block.sync
                def _(sp):
                    sp.sem_inc(row_free, CREDIT)
                    sp.sem_inc(mid_free, CREDIT)

                    def load(g, k, count, body):
                        sp.wait_ge(mid_done, free_at(count, BACK5[k]))
                        sp.dma_start(xin[:, k, :, :], node_rows(x, g)).then_inc(x_ready[k], 16)

                    def store_mid(g, k, count, body):
                        sp.wait_ge(mid_done, done_at(count))
                        sp.dma_start(node_rows(x_mid, g), mid[:, k, :, :]).then_inc(mid_stored[k], 16)

                    def mid_is_stored(g, k, count, body):
                        sp.wait_ge(mid_stored[k], body * 16 + 16)
                        sp.sem_inc(mid_free, 1)

                    def store_x1(g, k, count, body):
                        sp.wait_ge(row_done, done_at(count))
                        sp.dma_start(node_rows(rows_x1, g), row[:, k, :, :]).then_inc(row_stored[k], 16)

                    def store_pre(g, k, count, body):
                        sp.wait_ge(pre_kept, done_at(count))
                        sp.dma_start(node_rows(rows_p, g), pre_rows(k)).then_inc(row_stored[k], 16)

                    def row_is_stored(g, k, count, body):
                        sp.wait_ge(row_stored[k], body * 16 + 16)
                        sp.sem_inc(row_free, 1)

                    if last:
                        skewed(sp, GBODIES, None, [(load, 0), (store_mid, 2), (mid_is_stored, 3),
                                                   (store_pre, 3), (row_is_stored, 4)])
                    else:
                        skewed(sp, GBODIES, None, [(store_x1, 0), (row_is_stored, 1)])

                @block.tensor
                def _(pe):
                    pe.sem_inc(y_done, CREDIT)
                    pe.sem_inc(turned, CREDIT)
                    pe.sem_inc(pre_done, CREDIT)

                    def project(g, k, count, body):
                        pe.wait_ge(y_t_done, free_at(count, back_p[k]))
                        to = p_proj[:, ring_p[k], 0:GN]
                        pe.matmul(to, wa[:, layer, :], columns(feat, D1, g), start=True, stop=False)
                        pe.matmul(to, wb[:, layer, :], columns(sums, D1, g), start=False, stop=True)\
                            .then_inc(proj_done, 1)

                    def to_rows(g, k, count, body):
                        pe.wait_ge(y_t_done, done_at(count))
                        pe.wait_ge(y_used, free_at(count, BACK2[k]))
                        for b in range(BL):
                            i = pe.transpose(p_y[:, RING2[k], b * D:(b + 1) * D],
                                             y_t[:, RING2[k], b * NB:(b + 1) * NB], ident[0:D, 0:D])
                        i.then_inc(y_done, 1)

                    def turn(g, k, count, body):
                        pe.wait_ge(row_done, done_at(count))
                        pe.wait_ge(feat_done, free_at(count, BACK2[k]))
                        for b in range(BL):
                            i = pe.transpose(p_turn[:, RING2[k], b * NB:(b + 1) * NB], row[:, k, b, :],
                                             ident[0:NB, 0:NB])
                        i.then_inc(turned, 1)

                    def table(g, k, count, body):
                        pe.wait_ge(turned_kept, count + 1)
                        pe.wait_ge(pre_kept, free_at(count, 1))
                        for b in range(BL):
                            i = pe.matmul(p_pre[:, b // 2, b % 2 * 2 * D:(b % 2 + 1) * 2 * D],
                                          turned_s[:, RING2[k], b * NB:(b + 1) * NB], w_pre[:, :],
                                          start=True, stop=True)
                        i.then_inc(pre_done, 1)

                    if last:
                        pe.wait_ge(ones_set, 1)
                        hold(pe)
                        skewed(pe, GBODIES, None, [(project, 0), (to_rows, 1), (turn, 3), (table, 4)])
                    else:
                        skewed(pe, GBODIES, None, [(project, 0), (to_rows, 1), (turn, 2)])

                @block.scalar
                def _(act):
                    act.sem_inc(y_t_done, CREDIT)
                    act.sem_inc(std_done, CREDIT)
                    act.sem_inc(std2_done, CREDIT)
                    act.sem_inc(feat_done, CREDIT)
                    act.sem_inc(pre_kept, CREDIT)
                    if last:
                        act.sem_inc(row_done, CREDIT)

                    def copy_y(g, k, count, body):
                        act.wait_ge(proj_done, count + 1)
                        act.wait_ge(y_done, free_at(count, BACK2[k]))
                        act.activation(y_t[:, RING2[k], :], p_proj[:, ring_p[k], 0:GN], ACT.Copy)\
                            .then_inc(y_t_done, 1)

                    def root(g, k, count, body):
                        act.wait_ge(var_done, count + 1)
                        act.wait_ge(y_used, free_at(count, BACK5[k]))
                        act.activation(std[:, k, :], mean_var[:, k, :, 1], ACT.Sqrt,
                                       scale=D / (D - 1)).then_inc(std_done, 1)

                    def root2(g, k, count, body):
                        act.wait_ge(var2_done, count + 1)
                        act.wait_ge(norm_done, free_at(count, BACK5[k]))
                        act.activation(std2[:, k, :], mean_var2[:, k, :, 1], ACT.Sqrt,
                                       bias=eps_col[:, :]).then_inc(std2_done, 1)

                    def relu(g, k, count, body):
                        act.wait_ge(norm_done, done_at(count))
                        act.activation(row[:, k, :, :], row[:, k, :, :], ACT.Relu).then_inc(row_done, 1)

                    def keep(g, k, count, body):
                        act.wait_ge(turned, done_at(count))
                        if last:
                            act.wait_ge(pre_done, free_at(count, BACK2[k]))
                            act.activation(turned_s[0:D, RING2[k], :], p_turn[:, RING2[k], 0:GN],
                                           ACT.Copy).then_inc(turned_kept, 1)
                        act.activation(columns(feat, D, g), p_turn[:, RING2[k], 0:GN], ACT.Copy)\
                            .then_inc(feat_done, 1)

                    def keep_pre(g, k, count, body):
                        act.wait_ge(pre_done, done_at(count))
                        act.wait_ge(row_free, free_at(count, BACK5[k]))
                        four = got[0:NB, k, 0:8 * D].rearrange("p (b f) -> p b f", b=2)
                        act.activation(four, p_pre[:, 0:2, 0:4 * D], ACT.Copy)
                        act.activation(got[0:NB, k, 8 * D:10 * D], p_pre[:, 2, 0:2 * D], ACT.Copy)\
                            .then_inc(pre_kept, 1)

                    if last:
                        skewed(act, GBODIES, None, [(copy_y, 0), (root, 1), (root2, 2), (relu, 3),
                                                    (keep, 4), (keep_pre, 5)])
                    else:
                        skewed(act, GBODIES, None, [(copy_y, 0), (root, 1), (keep, 2)])

                @block.vector
                def _(dve):
                    if last:
                        dve.sem_inc(scaled, CREDIT)
                        dve.sem_inc(mid_done, CREDIT)
                        dve.sem_inc(norm_done, CREDIT)
                        dve.memset(turned_s[D:D1, :, :], 1.0).then_inc(ones_set, 1)
                    else:
                        dve.sem_inc(row_done, CREDIT)

                    def statistics(g, k, count, body):
                        dve.wait_ge(y_done, done_at(count))
                        dve.wait_ge(std_done, free_at(count, BACK5[k]))
                        for b in range(BL):
                            dve.bn_stats(stat[:, k, b, :], p_y[:, RING2[k], b * D:(b + 1) * D])\
                                .then_inc(stat_done, 1)
                        dve.wait_ge(stat_done, count * BL + BL)
                        hold(dve)
                        for b in range(BL):
                            i = dve.bn_aggr(mean_var[:, k, b, :], stat[:, k, b, :])
                        i.then_inc(var_done, 1)

                    def y_rows(k):
                        return p_y[:, RING2[k], 0:BL * D].rearrange("p (b f) -> p b f", f=D)

                    def scale(g, k, count, body):
                        dve.wait_ge(std_done, done_at(count))
                        dve.reciprocal(std[:, k, :], std[:, k, :]).then_inc(rstd_done, 1)
                        dve.wait_ge(row_free, free_at(count, BACK5[k]))
                        dve.wait_ge(turned, free_at(count, BACK5[k]))
                        dve.wait_ge(rstd_done, count + 1)
                        dve.tensor_tensor(row[:, k, :, :], y_rows(k), over(std[:, k, :]), ALU.mult)\
                            .then_inc(row_done, 1)

                    def residual(g, k, count, body):
                        dve.wait_ge(std_done, done_at(count))
                        dve.reciprocal(std[:, k, :], std[:, k, :]).then_inc(rstd_done, 1)
                        dve.wait_ge(mid_free, free_at(count, BACK5[k]))
                        dve.wait_ge(rstd_done, count + 1)
                        dve.tensor_tensor(mid[:, k, :, :], y_rows(k), over(std[:, k, :]), ALU.mult)\
                            .then_inc(scaled, 1)
                        dve.wait_ge(x_ready[k], body * 16 + 16)
                        dve.wait_ge(scaled, done_at(count))
                        dve.tensor_tensor(mid[:, k, :, :], mid[:, k, :, :], xin[:, k, :, :], ALU.add)\
                            .then_inc(mid_done, 1)
                        dve.wait_ge(std2_done, free_at(count, BACK5[k]))
                        dve.wait_ge(mid_done, done_at(count))
                        for b in range(BL):
                            dve.bn_stats(stat2[:, k, b, :], mid[:, k, b, :]).then_inc(stat2_done, 1)
                        dve.wait_ge(stat2_done, count * BL + BL)
                        hold(dve)
                        for b in range(BL):
                            i = dve.bn_aggr(mean_var2[:, k, b, :], stat2[:, k, b, :])
                        i.then_inc(var2_done, 1)

                    def normalise(g, k, count, body):
                        dve.wait_ge(var2_done, count + 1)
                        dve.wait_ge(turned, free_at(count, BACK5[k]))
                        dve.tensor_tensor(row[:, k, :, :], mid[:, k, :, :],
                                          over(mean_var2[:, k, :, 0]), ALU.subtract)\
                            .then_inc(cent_done, 1)
                        dve.wait_ge(std2_done, done_at(count))
                        dve.reciprocal(std2[:, k, :], std2[:, k, :]).then_inc(rstd2_done, 1)
                        dve.wait_ge(cent_done, count + 1)
                        dve.wait_ge(rstd2_done, count + 1)
                        dve.tensor_tensor(row[:, k, :, :], row[:, k, :, :], over(std2[:, k, :]),
                                          ALU.mult).then_inc(norm_done, 1)

                    if last:
                        skewed(dve, GBODIES, None, [(residual, 1), (normalise, 2), (statistics, 0)])
                    else:
                        skewed(dve, GBODIES, None, [(scale, 1), (statistics, 0)])

        def node_update():
            with ExitStack() as own:
                names, slots = semaphores(own)

                def tmp(n, shape):
                    return own.enter_context(nc.sbuf_tensor("n3_" + n, shape, F32))

                def ps(n, shape):
                    return own.enter_context(nc.psum_tensor("n3_" + n, shape, F32))

                hidden = tmp("hidden", [D, 2, GN])
                upd = tmp("upd", [D, 2, GN])
                stat = tmp("stat", [NB, 5, BL, 6])
                mean_var = tmp("mv", [NB, 5, BL, 2])
                std = tmp("std", [NB, 5, BL])
                cent = spare
                p_hidden = ps("p_hidden", [D, 2, 512])
                p_upd = ps("p_upd", [D, 2, 512])
                p_y = ps("p_y", [NB, 2, 512])
                x_ready, out_stored = slots("n3_x_ready"), slots("n3_out_stored")
                (up_done, gelu_done, down_done, upd_done, y_done, stat_done, var_done, std_done,
                 rstd_done, cent_done, steps, out_done, out_free) = names(
                    *("n3_" + n for n in ("up_done", "gelu_done", "down_done", "upd_done", "y_done",
                                          "stat_done", "var_done", "std_done", "rstd_done",
                                          "cent_done", "steps", "out_done", "out_free")))
                block = own.enter_context(nc.Block())

                @block.sync
                def _(sp):
                    sp.sem_inc(out_free, CREDIT)

                    def load(g, k, count, body):
                        sp.wait_ge(out_done, free_at(count, BACK5[k]))
                        sp.dma_start(xin[:, k, :, :], node_rows(x_mid, g)).then_inc(x_ready[k], 16)

                    def store(g, k, count, body):
                        sp.wait_ge(out_done, done_at(count))
                        sp.dma_start(node_rows(out, g), row[:, k, :, :]).then_inc(out_stored[k], 16)

                    def stored(g, k, count, body):
                        sp.wait_ge(out_stored[k], body * 16 + 16)
                        sp.sem_inc(out_free, 1)

                    skewed(sp, GBODIES, None, [(load, 0), (store, 3), (stored, 4)])

                @block.tensor
                def _(pe):
                    pe.sem_inc(down_done, CREDIT)
                    pe.sem_inc(y_done, CREDIT)

                    def up(g, k, count, body):
                        pe.wait_ge(gelu_done, free_at(count, BACK2[k]))
                        to = p_hidden[:, RING2[k], 0:GN]
                        pe.matmul(to, wu_self[:, :], columns(feat, D1, g), start=True, stop=False)
                        pe.matmul(to, wu_sum[:, :], columns(sums, D1, g), start=False, stop=True)\
                            .then_inc(up_done, 1)

                    def down(g, k, count, body):
                        pe.wait_ge(gelu_done, done_at(count))
                        pe.wait_ge(upd_done, free_at(count, BACK2[k]))
                        to = p_upd[:, RING2[k], 0:GN]
                        pe.matmul(to, uw2[:, :], hidden[:, RING2[k], :], start=True, stop=False)
                        pe.matmul(to, ident[0:D, 0:D], columns(feat, D, g), start=False, stop=True)\
                            .then_inc(down_done, 1)

                    def to_rows(g, k, count, body):
                        pe.wait_ge(upd_done, done_at(count))
                        pe.wait_ge(cent_done, free_at(count, BACK2[k]))
                        for b in range(BL):
                            i = pe.transpose(p_y[:, RING2[k], b * D:(b + 1) * D],
                                             upd[:, RING2[k], b * NB:(b + 1) * NB], ident[0:D, 0:D])
                        i.then_inc(y_done, 1)

                    skewed(pe, GBODIES, None, [(up, 0), (down, 1), (to_rows, 2)])

                @block.scalar
                def _(act):
                    act.sem_inc(gelu_done, CREDIT)
                    act.sem_inc(upd_done, CREDIT)
                    act.sem_inc(std_done, CREDIT)

                    def gelu(g, k, count, body):
                        act.wait_ge(up_done, count + 1)
                        act.wait_ge(down_done, free_at(count, BACK2[k]))
                        act.activation(hidden[:, RING2[k], :], p_hidden[:, RING2[k], 0:GN], ACT.Gelu)\
                            .then_inc(gelu_done, 1)

                    def copy_upd(g, k, count, body):
                        act.wait_ge(down_done, done_at(count))
                        act.wait_ge(y_done, free_at(count, BACK2[k]))
                        act.activation(upd[:, RING2[k], :], p_upd[:, RING2[k], 0:GN], ACT.Identity,
                                       bias=ub2_col[:, :]).then_inc(upd_done, 1)

                    def root(g, k, count, body):
                        act.wait_ge(var_done, count + 1)
                        act.wait_ge(out_done, free_at(count, BACK5[k]))
                        act.activation(std[:, k, :], mean_var[:, k, :, 1], ACT.Sqrt,
                                       bias=eps_col[:, :]).then_inc(std_done, 1)

                    skewed(act, GBODIES, None, [(gelu, 0), (copy_upd, 1), (root, 3)])

                @block.vector
                def _(dve):
                    dve.sem_inc(cent_done, CREDIT)
                    dve.sem_inc(out_done, CREDIT)

                    def centre(g, k, count, body):
                        dve.wait_ge(y_done, done_at(count))
                        dve.wait_ge(std_done, free_at(count, BACK5[k]))
                        for b in range(BL):
                            dve.bn_stats(stat[:, k, b, :], p_y[:, RING2[k], b * D:(b + 1) * D])\
                                .then_inc(stat_done, 1)
                        dve.wait_ge(stat_done, count * BL + BL)
                        hold(dve)
                        for b in range(BL):
                            i = dve.bn_aggr(mean_var[:, k, b, :], stat[:, k, b, :])
                        i.then_inc(var_done, 1)
                        dve.wait_ge(var_done, count + 1)
                        dve.tensor_tensor(cent[:, k, :, :],
                                          p_y[:, RING2[k], 0:BL * D].rearrange("p (b f) -> p b f", f=D),
                                          over(mean_var[:, k, :, 0]), ALU.subtract)\
                            .then_inc(cent_done, 1)

                    def finish(g, k, count, body):
                        c = cent[:, k, :, :]
                        dve.wait_ge(std_done, done_at(count))
                        dve.reciprocal(std[:, k, :], std[:, k, :]).then_inc(rstd_done, 1)
                        dve.wait_ge(rstd_done, count + 1)
                        dve.wait_ge(cent_done, done_at(count))
                        dve.tensor_tensor(c, c, over(std[:, k, :]), ALU.mult).then_inc(steps, 1)
                        dve.wait_ge(steps, count * 3 + 1)
                        dve.tensor_tensor(c, c, lng_row[:, :].unsqueeze(1).broadcast_to([NB, BL, D]),
                                          ALU.mult).then_inc(steps, 1)
                        dve.wait_ge(steps, count * 3 + 2)
                        dve.tensor_tensor(c, c, lnb_row[:, :].unsqueeze(1).broadcast_to([NB, BL, D]),
                                          ALU.add).then_inc(steps, 1)
                        dve.wait_ge(steps, count * 3 + 3)
                        dve.wait_ge(x_ready[k], body * 16 + 16)
                        dve.wait_ge(out_free, free_at(count, BACK5[k]))
                        dve.tensor_tensor(row[:, k, :, :], c, xin[:, k, :, :], ALU.add)\
                            .then_inc(out_done, 1)

                    skewed(dve, GBODIES, None, [(centre, 0), (finish, 2)])

        node_norm_first()
        linear_pass("l0", rows_h)
        node_layer("n1_", 0, False)
        linear_pass("l1", rows_x1)
        node_layer("n2_", 1, True)
        gated_pass("g", rows_p)
        node_update()


def kernel(**inputs):
    import numpy as np
    import concourse.bacc as bacc
    from concourse.bass_utils import run_bass_kernel_spmd

    a = {name: np.asarray(value) for name, value in inputs.items()}
    g = {name[len("L1_gnn_"):]: value for name, value in a.items() if name.startswith("L1_gnn_")}
    l = {name[len("L0_gnn_"):]: value for name, value in a.items() if name.startswith("L0_gnn_")}
    laid = {
        "x": a["x"],
        "src": a["src"].reshape(CHUNKS, TILES, P).transpose(0, 2, 1),
        "dst_tiles": a["dst"].reshape(CHUNKS * TILES, P).T,
        "dst_rows": a["dst"].reshape(BODIES, UNROLL, CE),
        "edge_t": a["edge_attr_32"].T,
        "W0T": l["W0"].transpose(0, 2, 1), "b0": l["b0"].reshape(2, D, 1),
        "W1T": l["W1"].transpose(0, 2, 1), "b1": l["b1"].reshape(2, D, 1),
        "W2": l["W2"], "b2": l["b2"].reshape(2, 1, D),
        "mW1": g["mW1"], "mb1": g["mb1"].reshape(1, D), "mW2T": g["mW2"].T, "mb2": g["mb2"].reshape(D, 1),
        "gW1": g["gW1"], "gb1": g["gb1"].reshape(1, D), "gW2": g["gW2"].reshape(D), "gb2": g["gb2"],
        "uW1": g["uW1"], "ub1": g["ub1"].reshape(1, D), "uW2": g["uW2"], "ub2": g["ub2"].reshape(D, 1),
        "ln_g": g["ln_g"], "ln_b": g["ln_b"],
    }
    nc = bacc.Bacc("TRN2", target_bir_lowering=False, num_devices=1)
    arrays, args = {}, []
    for name, value in laid.items():
        value = np.ascontiguousarray(value)
        arrays[f"in_{name}"] = value
        args.append(nc.dram_tensor(f"in_{name}", value.shape, mybir.dt.from_np(value.dtype),
                                   kind="ExternalInput").ap())
    args.append(nc.dram_tensor("out", (N, D), F32, kind="ExternalOutput").ap())
    for name, shape in (("rows_h", (N, D)), ("rows_x1", (N, D)), ("rows_p", (N, 2 * D)),
                        ("x_mid", (N, D)), ("extents", (2, BODIES, UNROLL))):
        args.append(nc.dram_tensor(name, shape, F32, kind="Internal").ap())
    gnn(nc, *args)
    r = run_bass_kernel_spmd(nc, [arrays], core_ids=[0])
    return r.results[0]["out"]
```

```python
import concourse.bass as bass
from concourse import mybir
from contextlib import ExitStack

F32 = mybir.dt.float32
I32 = mybir.dt.int32
ALU = mybir.AluOpType
ACT = mybir.ActivationFunctionType
AX = mybir.AxisListType

N, E, D, ED = 12500, 400000, 96, 32
D1 = D + 1
P = 128
EPS = 1e-5

UNROLL = 5
TILES = 5
CE = TILES * P
CHUNKS = E // CE
BODIES = CHUNKS // UNROLL
WIN_BITS = 6
WIN = 1 << WIN_BITS
ROUNDS_MAX = (N - 1) // WIN + 1

NB = 100
BL = 5
GN = NB * BL
GROUPS = N // GN
GBODIES = GROUPS // UNROLL
assert CHUNKS * CE == E and BODIES * UNROLL == CHUNKS and GBODIES * UNROLL * GN == N

RING5, BACK5 = [0, 1, 2, 3, 4], [5, 5, 5, 5, 5]
RING2, BACK2 = [0, 1, 0, 1, 0], [1, 3, 2, 2, 2]
RING1, BACK1 = [0] * 5, [1] * 5
CREDIT = 5


def free_at(count, back):
    return count + (CREDIT + 1 - back)


def done_at(count):
    return count + (CREDIT + 1)


def skewed(eng, bodies, before, stages):
    most = max(skew for _, skew in stages)
    peeled = max(1, -(-most // UNROLL))

    def emit(first, k, skew, stage):
        back = -(-max(skew - k, 0) // UNROLL)
        body = first - back if back else first
        kk = k - skew + UNROLL * back
        total = body + before if before is not None else body
        stage(body * UNROLL + kk, kk, total * UNROLL + kk, total)

    for item in range(peeled * UNROLL):
        for stage, skew in stages:
            if item >= skew:
                emit(item // UNROLL, item % UNROLL, skew, stage)
    with eng.Fori(peeled, bodies) as b:
        for k in range(UNROLL):
            for stage, skew in stages:
                emit(b, k, skew, stage)
    for item in range(most):
        for stage, skew in stages:
            if item < skew:
                emit(bodies + item // UNROLL, item % UNROLL, skew, stage)


def gnn(nc, x, src, dst_tiles, dst_rows, edge_t, W0T, b0, W1T, b1, W2, b2, mW1, mb1, mW2T, mb2,
        gW1, gb1, gW2, gb2, uW1, ub1, uW2, ub2, ln_g, ln_b, out,
        rows_h, rows_x1, rows_p, x_mid, extents):
    ctx = ExitStack()
    with ctx:
        def sb(name, shape, dt=F32):
            return ctx.enter_context(nc.sbuf_tensor(name, shape, dt))

        feat = sb("feat", [D1, N])
        sums = sb("sums", [P, N + WIN])
        dst_rel = sb("dst_rel", [P, CHUNKS * TILES])
        start0 = sb("start0", [1, CHUNKS])
        start_f = sb("start_f", [1, CHUNKS])
        start_i = sb("start_i", [1, CHUNKS], I32)
        rounds_i = sb("rounds_i", [P, 1], I32)
        rounds_w = sb("rounds_w", [P, 1])
        ident = sb("ident", [P, P])
        window = sb("window", [P, WIN])
        wa = sb("wa", [D1, 2, D])
        wb = sb("wb", [D1, 2, D])
        w_pre = sb("w_pre", [D1, 2 * D])
        w_edge = sb("w_edge", [ED, 2 * D])
        wu_self = sb("wu_self", [D1, D])
        wu_sum = sb("wu_sum", [D1, D])
        uw2 = sb("uw2", [D, D])
        ub2_col = sb("ub2_col", [D, 1])
        gw2_row = sb("gw2_row", [P, D])
        gb2_half = sb("gb2_half", [P, 1])
        lng_row = sb("lng_row", [NB, D])
        lnb_row = sb("lnb_row", [NB, D])
        eps_col = sb("eps_col", [NB, 1])
        idx = sb("idx", [P, 5, TILES], I32)
        got = sb("got", [P, 5, TILES * 2 * D])
        hot = sb("hot", [P, 5, TILES, WIN])
        msg = sb("msg", [P, 5, TILES, D1])
        edge_room = sb("edge_room", [P, 5, CE])
        edge = edge_room[0:ED, :, :]
        zz = sb("zz", [P, 5, TILES])
        gate = sb("gate", [P, 5, TILES])
        spare = edge_room[0:NB, :, 0:BL * D].rearrange("p k (b f) -> p k b f", f=D)
        xin = sb("xin", [NB, 5, BL, D])
        row = sb("row", [NB, 5, BL, D])

        def semaphores(own):
            used = []

            def name(n):
                used.append(nc.alloc_semaphore(name=n))
                return used[-1]

            def clear():
                nc.clear_and_free_semaphores(used)
                nc.all_engine_barrier()

            own.callback(clear)
            return (lambda *list_: [name(n) for n in list_]), (lambda n: [name(f"{n}{k}") for k in range(5)])

        passed = ctx.enter_context(nc.semaphore("passed"))

        def hold(eng):
            eng.sem_inc(passed, 1)

        def node_rows(table, g):
            return table[bass.ds(g * GN, GN), :].rearrange("(b p) f -> p b f", p=NB)

        def columns(t, rows, g):
            return t[0:rows, bass.ds(g * GN, GN)]

        def over(col, width=D):
            return col.unsqueeze(2).broadcast_to([NB, BL, width])

        def node_norm_first():
            with ExitStack() as own:
                names, slots = semaphores(own)

                def ps(name, shape):
                    return own.enter_context(nc.psum_tensor(name, shape, F32))

                def tmp(name, shape, dt=F32):
                    return own.enter_context(nc.sbuf_tensor(name, shape, dt))

                w0t = tmp("w0t", [D, 2, D1])
                w1t = tmp("w1t", [D, 2, D1])
                mw2t = tmp("mw2t", [D, D1])
                w2a = tmp("w2a", [D, 2, D])
                w2b = tmp("w2b", [D, 2, D])
                uw1b = tmp("uw1b", [D, D])
                b2r = tmp("b2r", [1, 2, D])
                last_row = tmp("last_row", [1, D1])
                lo = tmp("lo", [BODIES, UNROLL])
                hi = tmp("hi", [BODIES, UNROLL])
                starts = tmp("starts", [P, CHUNKS])
                window_i = tmp("window_i", [P, WIN], I32)
                widest = tmp("widest", [P, 4])
                widest_i = tmp("widest_i", [P, 2], I32)
                dst_i = got[:, :, :].rearrange("p a b -> p (a b)")[:, 0:CHUNKS * TILES].bitcast(I32)
                dst_c = sums[0:BODIES, 0:UNROLL * CE].bitcast(I32).rearrange("p (u e) -> p u e", u=UNROLL)
                his = hot[:, 0:2, :, :].rearrange("p a b c -> p (a b c)")[:, 0:CHUNKS]
                stat = tmp("n0_stat", [NB, 5, BL, 6])
                mean_var = tmp("n0_mv", [NB, 5, BL, 2])
                std = tmp("n0_std", [NB, 5, BL])
                shift = tmp("n0_shift", [NB, 5, BL])
                p_w = ps("p_w", [D1, 5, 512])
                p_t = ps("n0_pt", [D, 2, 512])
                (w_in, halved, w_mul, w_out, dst_in, tiles_in, iota_done, sel_set, ext_out, ext_in,
                 min_done, wide, rel_done, consts, ones_done) = names(
                    "w_in", "halved", "w_mul", "w_out", "dst_in", "tiles_in", "iota_done", "sel_set",
                    "ext_out", "ext_in", "min_done", "wide", "rel_done", "consts",
                    "ones_done")
                x_ready, row_stored = slots("n0_x_ready"), slots("n0_stored")
                (stat_done, var_done, std_done, rstd_done, norm_done, row_done, turned, row_free,
                 feat_done) = names(*("n0_" + n for n in (
                     "stat_done", "var_done", "std_done", "rstd_done", "norm_done", "row_done",
                     "turned", "row_free", "feat_done")))
                loads = [(w_pre[0:D, 0:D], mW1[0:D, :]), (w_pre[0:D, D:2 * D], gW1[0:D, :]),
                         (w_pre[D:D1, 0:D], mb1), (w_pre[D:D1, D:2 * D], gb1),
                         (w_edge[:, 0:D], mW1[D:D + ED, :]), (w_edge[:, D:2 * D], gW1[D:D + ED, :]),
                         (wu_self[0:D, :], uW1[0:D, :]), (wu_self[D:D1, :], ub1),
                         (uw1b[:, :], uW1[D:2 * D, :]), (uw2[:, :], uW2), (ub2_col[:, :], ub2),
                         (gw2_row[:, :], gW2.partition_broadcast(P)),
                         (gb2_half[:, :], gb2.partition_broadcast(P)),
                         (lng_row[:, :], ln_g.partition_broadcast(NB)),
                         (lnb_row[:, :], ln_b.partition_broadcast(NB)),
                         (mw2t[:, 0:D], mW2T), (mw2t[:, D:D1], mb2)]
                for i in range(2):
                    loads += [(w0t[:, i, 0:D], W0T[i]), (w0t[:, i, D:D1], b0[i]),
                              (w1t[:, i, 0:D], W1T[i]), (w1t[:, i, D:D1], b1[i]),
                              (w2a[:, i, :], W2[i, 0:D, :]), (w2b[:, i, :], W2[i, D:2 * D, :]),
                              (b2r[:, i, :], b2[i])]
                block = own.enter_context(nc.Block())

                @block.sync
                def _(sp):
                    sp.sem_inc(row_free, CREDIT)

                    def load(g, k, count, body):
                        sp.wait_ge(row_done, free_at(count, BACK5[k]))
                        sp.dma_start(xin[:, k, :, :], node_rows(x, g)).then_inc(x_ready[k], 16)

                    def store(g, k, count, body):
                        sp.wait_ge(row_done, done_at(count))
                        sp.dma_start(node_rows(rows_h, g), row[:, k, :, :]).then_inc(row_stored[k], 16)

                    def stored(g, k, count, body):
                        sp.wait_ge(row_stored[k], 16 * (body + 1))
                        sp.sem_inc(row_free, 1)

                    skewed(sp, GBODIES, None, [(load, 0), (store, 3), (stored, 4)])

                @block.gpsimd
                def _(pool):
                    pool.memset(ident[:, :], 0.0).then_inc(sel_set, 1)
                    pool.wait_ge(sel_set, 1)
                    pool.affine_select(out=ident[:, :], in_=ident[:, :], compare_op=ALU.not_equal,
                                       fill=1.0, base=0, pattern=[[-1, P]], channel_multiplier=1)\
                        .then_inc(sel_set, 1)
                    pool.iota(window_i[:, :], pattern=[[1, WIN]], base=0, channel_multiplier=0)\
                        .then_inc(iota_done, 1)
                    pool.dma_start(dst_c, dst_rows).then_inc(dst_in, 16)
                    pool.dma_start(dst_i, dst_tiles).then_inc(tiles_in, 16)
                    pool.wait_ge(iota_done, 1)
                    pool.memset(feat[D:D1, :], 1.0).then_inc(ones_done, 1)
                    pool.wait_ge(min_done, 2)
                    pool.dma_start(extents[0], lo[:, :]).then_inc(ext_out, 16)
                    pool.dma_start(extents[1], hi[:, :]).then_inc(ext_out, 16)
                    pool.wait_ge(ext_out, 32)
                    flat = extents.rearrange("a b u -> a (b u)")
                    pool.dma_start(starts[:, :], flat[0:1, :].partition_broadcast(P)).then_inc(ext_in, 16)
                    pool.dma_start(his, flat[1:2, :].partition_broadcast(P)).then_inc(ext_in, 16)
                    pool.wait_ge(ext_in, 32)
                    pool.wait_ge(ones_done, 1)

                @block.vector
                def _(dve):
                    dve.memset(last_row[:, :], 0.0).then_inc(consts, 1)
                    dve.memset(msg[:, :, :, D:D1], 1.0).then_inc(consts, 1)
                    dve.memset(eps_col[:, :], EPS).then_inc(consts, 1)
                    dve.wait_ge(consts, 3)
                    dve.memset(last_row[:, D:D1], 1.0).then_inc(consts, 1)
                    dve.wait_ge(iota_done, 1)
                    dve.tensor_copy(window[:, :], window_i[:, :]).then_inc(iota_done, 1)
                    dve.wait_ge(iota_done, 2)
                    dve.wait_ge(dst_in, 16)
                    dve.tensor_reduce(lo[:, :], dst_c, AX.X, ALU.min).then_inc(min_done, 1)
                    dve.tensor_reduce(hi[:, :], dst_c, AX.X, ALU.max).then_inc(min_done, 1)
                    dve.sem_inc(norm_done, CREDIT)
                    dve.sem_inc(feat_done, CREDIT)

                    def statistics(g, k, count, body):
                        dve.wait_ge(x_ready[k], 16 * (body + 1))
                        dve.wait_ge(std_done, free_at(count, BACK5[k]))
                        for b in range(BL):
                            dve.bn_stats(stat[:, k, b, :], xin[:, k, b, :]).then_inc(stat_done, 1)
                        dve.wait_ge(stat_done, count * BL + BL)
                        hold(dve)
                        for b in range(BL):
                            i = dve.bn_aggr(mean_var[:, k, b, :], stat[:, k, b, :])
                        i.then_inc(var_done, 1)

                    def shifts(g, k, count, body):
                        dve.wait_ge(std_done, done_at(count))
                        dve.reciprocal(std[:, k, :], std[:, k, :]).then_inc(rstd_done, 1)
                        dve.wait_ge(rstd_done, count + 1)
                        dve.wait_ge(row_done, free_at(count, BACK5[k]))
                        dve.scalar_tensor_tensor(out=shift[:, k, :], in0=mean_var[:, k, :, 0],
                                                 scalar=-1.0, in1=std[:, k, :], op0=ALU.mult,
                                                 op1=ALU.mult).then_inc(norm_done, 1)

                    def keep(g, k, count, body):
                        dve.wait_ge(turned, count + 1)
                        dve.tensor_copy(columns(feat, D, g), p_t[:, RING2[k], 0:GN])\
                            .then_inc(feat_done, 1)

                    skewed(dve, GBODIES, None, [(statistics, 0), (shifts, 1), (keep, 3)])
                    dve.wait_ge(ext_in, 32)
                    dve.tensor_tensor(his, his, starts[:, :], ALU.subtract).then_inc(wide, 1)
                    dve.tensor_copy(start0[:, :], starts[0:1, :]).then_inc(wide, 1)
                    dve.tensor_copy(start_f[:, :], starts[0:1, :]).then_inc(wide, 1)
                    dve.tensor_copy(start_i[:, :], starts[0:1, :]).then_inc(wide, 1)
                    dve.wait_ge(wide, 4)
                    dve.tensor_reduce(widest[:, 0:1], his, AX.X, ALU.max).then_inc(wide, 1)
                    dve.wait_ge(wide, 5)
                    dve.tensor_copy(widest_i[:, 0:1], widest[:, 0:1]).then_inc(wide, 1)
                    dve.wait_ge(wide, 6)
                    dve.tensor_scalar(widest_i[:, 1:2], widest_i[:, 0:1], WIN_BITS, None,
                                      ALU.arith_shift_right).then_inc(wide, 1)
                    dve.wait_ge(wide, 7)
                    dve.tensor_scalar(widest[:, 1:2], widest_i[:, 1:2], 1.0, None, ALU.add).then_inc(wide, 1)
                    dve.wait_ge(wide, 8)
                    dve.tensor_copy(rounds_i[:, :], widest[:, 1:2]).then_inc(wide, 1)
                    dve.tensor_scalar(rounds_w[:, :], widest[:, 1:2], float(WIN), None, ALU.mult)\
                        .then_inc(wide, 1)
                    dve.wait_ge(wide, 10)
                    dve.wait_ge(tiles_in, 16)
                    dve.tensor_tensor(dst_rel[:, :].rearrange("p (c t) -> p c t", t=TILES),
                                      dst_i.rearrange("p (c t) -> p c t", t=TILES),
                                      starts[:, :].unsqueeze(2).broadcast_to([P, CHUNKS, TILES]),
                                      ALU.subtract).then_inc(rel_done, 1)
                    dve.wait_ge(rel_done, 1)

                @block.scalar
                def _(act):
                    for to, of in loads:
                        act.dma_start(to, of).then_inc(w_in, 16)
                    act.sem_inc(std_done, CREDIT)
                    act.sem_inc(row_done, CREDIT)
                    act.wait_ge(consts, 4)

                    def root(g, k, count, body):
                        act.wait_ge(var_done, count + 1)
                        act.wait_ge(norm_done, free_at(count, BACK5[k]))
                        act.activation(std[:, k, :], mean_var[:, k, :, 1], ACT.Sqrt,
                                       bias=eps_col[:, :]).then_inc(std_done, 1)

                    def relu(g, k, count, body):
                        act.wait_ge(norm_done, done_at(count))
                        act.wait_ge(row_free, free_at(count, BACK5[k]))
                        for b in range(BL):
                            i = act.activation(row[:, k, b, :], xin[:, k, b, :], ACT.Relu,
                                               scale=std[:, k, b:b + 1], bias=shift[:, k, b:b + 1])
                        i.then_inc(row_done, 1)

                    skewed(act, GBODIES, None, [(root, 0), (relu, 1)])
                    act.wait_ge(w_in, 16 * len(loads))
                    act.mul(gb2_half[:, :], gb2_half[:, :], 0.5).then_inc(halved, 1)
                    act.wait_ge(w_mul, 1)
                    for n, to in enumerate((wa[:, 0, :], wa[:, 1, :], wb[:, 0, :], wb[:, 1, :], wu_sum[:, :])):
                        act.activation(to, p_w[:, n, 0:D], ACT.Copy).then_inc(w_out, 1)
                    act.wait_ge(w_out, 5)
                    act.wait_ge(halved, 1)

                @block.tensor
                def _(pe):
                    pe.wait_ge(sel_set, 2)

                    def turn(g, k, count, body):
                        pe.wait_ge(row_done, done_at(count))
                        pe.wait_ge(feat_done, free_at(count, BACK2[k]))
                        for b in range(BL):
                            i = pe.transpose(p_t[:, RING2[k], b * NB:(b + 1) * NB], row[:, k, b, :],
                                             ident[0:NB, 0:NB])
                        i.then_inc(turned, 1)

                    skewed(pe, GBODIES, None, [(turn, 0)])
                    pe.wait_ge(w_in, 16 * len(loads))
                    pe.wait_ge(consts, 4)
                    for i in range(2):
                        pe.matmul(p_w[:, i, 0:D], w1t[:, i, :], w2a[:, i, :], start=True, stop=False)
                        pe.matmul(p_w[:, i, 0:D], last_row[:, :], b2r[:, i, :], start=False, stop=True)
                        pe.matmul(p_w[:, 2 + i, 0:D], w0t[:, i, :], w2b[:, i, :], start=True, stop=True)
                    pe.matmul(p_w[:, 4, 0:D], mw2t[:, :], uw1b[:, :], start=True, stop=True).then_inc(w_mul, 1)

        def load_indices(sp, name, idx_ready, gathered, more=None):
            rounds = sp.value_load(rounds_i[0:1, 0:1], min_val=1, max_val=ROUNDS_MAX)
            for k in range(UNROLL):
                sp.dma_start(idx[:, k, :], src[k]).then_inc(idx_ready[k], 16)
                if more:
                    more(k, k, None)
            with sp.Fori(0, rounds) as r:
                with sp.Fori(1, BODIES) as b:
                    for k in range(UNROLL):
                        sp.wait_ge(gathered[k], (r * BODIES + b) * (16 * TILES))
                        sp.dma_start(idx[:, k, :], src[bass.ds(b * UNROLL + k, 1)].rearrange(
                            "c p t -> (c p) t")).then_inc(idx_ready[k], 16)
                        if more:
                            more(b * UNROLL + k, k, (r * BODIES + b) * UNROLL + k)
                for k in range(UNROLL):
                    sp.wait_ge(gathered[k], (r * BODIES + BODIES) * (16 * TILES))
                    sp.dma_start(idx[:, k, :], src[k]).then_inc(idx_ready[k], 16)
                    if more:
                        more(k, k, (r * BODIES + BODIES) * UNROLL + k)
            for k in range(UNROLL):
                sp.wait_ge(idx_ready[k], rounds * (16 * BODIES) + 16)
                hold(sp)


        def gather_rows(pool, table, width, pitch, idx_ready, gathered, free):
            rounds = pool.value_load(rounds_i[0:1, 0:1], min_val=1, max_val=ROUNDS_MAX)
            with pool.Fori(0, rounds) as r:
                with pool.Fori(0, BODIES) as b:
                    for k in range(UNROLL):
                        body = r * BODIES + b
                        pool.wait_ge(idx_ready[k], body * 16 + 16)
                        hold(pool)
                        pool.wait_ge(free, body * UNROLL + (k + 1))
                        hold(pool)
                        for t in range(TILES):
                            pool.indirect_dma_start(
                                got[:, k, t * pitch:t * pitch + width], None, table,
                                bass.IndirectOffsetOnAxis(idx[:, k, t:t + 1], axis=0))\
                                .then_inc(gathered[k], 16)

        def one_hot(dve, chunk, k):
            rel = dst_rel[:, bass.ds(chunk * TILES, TILES)].unsqueeze(2).broadcast_to([P, TILES, WIN])
            cols = window[:, :].unsqueeze(1).broadcast_to([P, TILES, WIN])
            return dve.tensor_tensor(hot[:, k, :, :], rel, cols, ALU.is_equal)

        def add_window(dve, chunk, p_seg_slot, start_reg):
            dve.reg_load(start_reg, start_i[0:1, bass.ds(chunk, 1)])
            start = dve.snap(start_reg, min_val=0, max_val=N)
            where = sums[0:D1, bass.ds(start, WIN)]
            return dve.tensor_tensor(where, where, p_seg_slot, ALU.add)

        def move_windows(dve, moved, r):
            dve.tensor_scalar(dst_rel[:, :], dst_rel[:, :], float(-WIN), None, ALU.add).then_inc(moved, 1)
            dve.tensor_scalar(start_f[:, :], start_f[:, :], float(WIN), None, ALU.add).then_inc(moved, 1)
            dve.wait_ge(moved, r * 3 + 2)
            dve.tensor_scalar(start_i[:, :], start_f[:, :], float(N), None, ALU.min).then_inc(moved, 1)
            dve.wait_ge(moved, r * 3 + 3)
            hold(dve)

        def restore_windows(dve, back):
            dve.tensor_scalar(dst_rel[:, :], dst_rel[:, :], rounds_w[:, 0:1], None, ALU.add).then_inc(back, 1)
            dve.tensor_copy(start_f[:, :], start0[:, :]).then_inc(back, 1)
            dve.tensor_copy(start_i[:, :], start0[:, :]).then_inc(back, 1)
            dve.wait_ge(back, 3)

        def linear_pass(name, table):
            with ExitStack() as own:
                names, slots = semaphores(own)
                p_seg = own.enter_context(nc.psum_tensor(name + "_seg", [D1, 5, 512], F32))
                idx_ready, gathered = slots(name + "_idx_ready"), slots(name + "_gathered")
                hot_done, seg_done, added, zeroed, moved, back = names(
                    name + "_hot_done", name + "_seg_done", name + "_added", name + "_zeroed",
                    name + "_moved", name + "_back")
                block = own.enter_context(nc.Block())

                def rows_of(k):
                    return got[:, k, 0:TILES * D1].rearrange("p (t f) -> p t f", f=D1)

                @block.sync
                def _(sp):
                    load_indices(sp, name, idx_ready, gathered)

                @block.gpsimd
                def _(pool):
                    gather_rows(pool, table, D, D1, idx_ready, gathered, seg_done)

                @block.tensor
                def _(pe):
                    pe.sem_inc(seg_done, CREDIT)
                    rounds = pe.value_load(rounds_i[0:1, 0:1], min_val=1, max_val=ROUNDS_MAX)
                    pe.wait_ge(zeroed, 1)
                    hold(pe)
                    with pe.Fori(0, rounds) as r:
                        def segment(chunk, k, count, body):
                            pe.wait_ge(gathered[k], body * (16 * TILES) + 16 * TILES)
                            pe.wait_ge(hot_done, count + 1)
                            pe.wait_ge(added, free_at(count, BACK5[k]))
                            for t in range(TILES):
                                i = pe.matmul(p_seg[:, k, 0:WIN], rows_of(k)[:, t, :], hot[:, k, t, :],
                                              start=t == 0, stop=t == TILES - 1)
                            i.then_inc(seg_done, 1)

                        skewed(pe, BODIES, r * BODIES, [(segment, 0)])

                @block.vector
                def _(dve):
                    dve.sem_inc(added, CREDIT)
                    rounds = dve.value_load(rounds_i[0:1, 0:1], min_val=1, max_val=ROUNDS_MAX)
                    start_reg = dve.alloc_register(name + "_start")
                    for k in range(5):
                        i = dve.memset(rows_of(k)[:, :, D:D1], 1.0)
                    i.then_inc(zeroed, 1)
                    dve.memset(sums[:, :], 0.0).then_inc(zeroed, 1)
                    dve.wait_ge(zeroed, 2)
                    hold(dve)
                    with dve.Fori(0, rounds) as r:
                        def hots(chunk, k, count, body):
                            dve.wait_ge(seg_done, free_at(count, BACK5[k]))
                            one_hot(dve, chunk, k).then_inc(hot_done, 1)

                        def add(chunk, k, count, body):
                            dve.wait_ge(seg_done, done_at(count))
                            dve.wait_ge(added, free_at(count, 1))
                            hold(dve)
                            add_window(dve, chunk, p_seg[:, k, 0:WIN], start_reg).then_inc(added, 1)

                        skewed(dve, BODIES, r * BODIES, [(hots, 0), (add, 1)])
                        move_windows(dve, moved, r)
                    restore_windows(dve, back)
                    dve.wait_ge(added, rounds * CHUNKS + CREDIT)
                    hold(dve)

        def gated_pass(name, table):
            with ExitStack() as own:
                names, slots = semaphores(own)
                p_edge = own.enter_context(nc.psum_tensor(name + "_edge", [P, 2, 3, 512], F32))
                p_seg = own.enter_context(nc.psum_tensor(name + "_seg", [D1, 2, 512], F32))
                idx_ready, gathered = slots(name + "_idx_ready"), slots(name + "_gathered")
                edge_ready = slots(name + "_edge_ready")
                (edge_done, pre_done, msg_done, gelu_done, z_done, tanh_done, gate_done, eq_done,
                 hot_done, seg_done, added, zeroed, moved, back) = names(
                    *(name + "_" + n for n in ("edge_done", "pre_done", "msg_done", "gelu_done",
                                               "z_done", "tanh_done", "gate_done", "eq_done",
                                               "hot_done", "seg_done", "added", "zeroed", "moved",
                                               "back")))
                block = own.enter_context(nc.Block())

                def halves(k):
                    return got[:, k, :].rearrange("p (t h f) -> p t h f", h=2, f=D)

                @block.sync
                def _(sp):
                    def attributes(chunk, k, count):
                        if count is None:
                            of = edge_t[:, chunk * CE:(chunk + 1) * CE]
                        else:
                            sp.wait_ge(edge_done, count - (UNROLL - 1))
                            of = edge_t[:, bass.ds(chunk * CE, CE)]
                        sp.dma_start(edge[:, k, :], of).then_inc(edge_ready[k], 16)

                    load_indices(sp, name, idx_ready, gathered, attributes)
                    rounds = sp.value_load(rounds_i[0:1, 0:1], min_val=1, max_val=ROUNDS_MAX)
                    for k in range(UNROLL):
                        sp.wait_ge(edge_ready[k], rounds * (16 * BODIES) + 16)
                        hold(sp)

                @block.gpsimd
                def _(pool):
                    gather_rows(pool, table, 2 * D, 2 * D, idx_ready, gathered, z_done)

                @block.tensor
                def _(pe):
                    pe.sem_inc(seg_done, CREDIT)
                    rounds = pe.value_load(rounds_i[0:1, 0:1], min_val=1, max_val=ROUNDS_MAX)
                    with pe.Fori(0, rounds) as r:
                        def edges(chunk, k, count, body):
                            pe.wait_ge(edge_ready[k], body * 16 + 16)
                            pe.wait_ge(pre_done, free_at(count, BACK2[k]))
                            for t in range(TILES):
                                i = pe.matmul(p_edge[:, RING2[k], t // 2, t % 2 * 2 * D:(t % 2 + 1) * 2 * D],
                                              edge[:, k, t * P:(t + 1) * P], w_edge[:, :],
                                              start=True, stop=True)
                            i.then_inc(edge_done, 1)

                        def segment(chunk, k, count, body):
                            pe.wait_ge(msg_done, count + 1)
                            pe.wait_ge(hot_done, count + 1)
                            pe.wait_ge(added, free_at(count, BACK2[k]))
                            for t in range(TILES):
                                i = pe.matmul(p_seg[:, RING2[k], 0:WIN], msg[:, k, t, :], hot[:, k, t, :],
                                              start=t == 0, stop=t == TILES - 1)
                            i.then_inc(seg_done, 1)

                        skewed(pe, BODIES, r * BODIES, [(edges, 0), (segment, 3)])

                @block.scalar
                def _(act):
                    rounds = act.value_load(rounds_i[0:1, 0:1], min_val=1, max_val=ROUNDS_MAX)
                    with act.Fori(0, rounds) as r:
                        def gelus(chunk, k, count, body):
                            act.wait_ge(pre_done, done_at(count))
                            act.activation(halves(k)[:, :, 1, :], halves(k)[:, :, 1, :], ACT.Gelu)\
                                .then_inc(gelu_done, 1)
                            act.wait_ge(seg_done, free_at(count, BACK5[k]))
                            act.activation(msg[:, k, :, 0:D], halves(k)[:, :, 0, :], ACT.Gelu)\
                                .then_inc(msg_done, 1)

                        def tanh(chunk, k, count, body):
                            act.wait_ge(z_done, done_at(count))
                            act.activation(gate[:, k, :], zz[:, k, :], ACT.Tanh, scale=0.5,
                                           bias=gb2_half[:, :]).then_inc(tanh_done, 1)

                        skewed(act, BODIES, r * BODIES, [(gelus, 0), (tanh, 1)])

                @block.vector
                def _(dve):
                    dve.sem_inc(pre_done, CREDIT)
                    dve.sem_inc(z_done, CREDIT)
                    dve.sem_inc(added, CREDIT)
                    rounds = dve.value_load(rounds_i[0:1, 0:1], min_val=1, max_val=ROUNDS_MAX)
                    start_reg = dve.alloc_register(name + "_start")
                    dve.memset(sums[:, :], 0.0).then_inc(zeroed, 1)
                    dve.wait_ge(zeroed, 1)
                    hold(dve)
                    with dve.Fori(0, rounds) as r:
                        def pre(chunk, k, count, body):
                            dve.wait_ge(gathered[k], body * (16 * TILES) + 16 * TILES)
                            dve.wait_ge(edge_done, count + 1)
                            four = got[:, k, 0:8 * D].rearrange("p (b f) -> p b f", b=2)
                            dve.tensor_tensor(four, four, p_edge[:, RING2[k], 0:2, 0:4 * D], ALU.add)
                            one = got[:, k, 8 * D:10 * D]
                            dve.tensor_tensor(one, one, p_edge[:, RING2[k], 2, 0:2 * D], ALU.add)\
                                .then_inc(pre_done, 1)

                        def gate_sums(chunk, k, count, body):
                            dve.wait_ge(gelu_done, count + 1)
                            dve.wait_ge(msg_done, count + 1)
                            for t in range(TILES):
                                half = halves(k)[:, t, 1, :]
                                i = dve.tensor_tensor_reduce(out=half, in0=half, in1=gw2_row[:, :],
                                                             scale=1.0, scalar=0.0, op0=ALU.mult,
                                                             op1=ALU.add, accum_out=zz[:, k, t:t + 1])
                            i.then_inc(z_done, 1)

                        def gated_hots(chunk, k, count, body):
                            dve.wait_ge(seg_done, free_at(count, BACK5[k]))
                            one_hot(dve, chunk, k).then_inc(eq_done, 1)
                            dve.wait_ge(tanh_done, count + 1)
                            dve.tensor_scalar(gate[:, k, :], gate[:, k, :], 0.5, 0.5, ALU.mult,
                                              ALU.add).then_inc(gate_done, 1)
                            dve.wait_ge(eq_done, count + 1)
                            dve.wait_ge(gate_done, count + 1)
                            dve.tensor_tensor(hot[:, k, :, :], hot[:, k, :, :],
                                              gate[:, k, :].unsqueeze(2).broadcast_to([P, TILES, WIN]),
                                              ALU.mult).then_inc(hot_done, 1)

                        def add(chunk, k, count, body):
                            dve.wait_ge(seg_done, done_at(count))
                            dve.wait_ge(added, free_at(count, 1))
                            hold(dve)
                            add_window(dve, chunk, p_seg[:, RING2[k], 0:WIN], start_reg).then_inc(added, 1)

                        skewed(dve, BODIES, r * BODIES,
                               [(pre, 0), (gate_sums, 1), (gated_hots, 2), (add, 3)])
                        move_windows(dve, moved, r)
                    restore_windows(dve, back)
                    dve.wait_ge(added, rounds * CHUNKS + CREDIT)
                    hold(dve)

        def node_layer(name, layer, last):
            with ExitStack() as own:
                names, slots = semaphores(own)

                def tmp(n, shape):
                    return own.enter_context(nc.sbuf_tensor(name + n, shape, F32))

                def ps(n, shape):
                    return own.enter_context(nc.psum_tensor(name + n, shape, F32))

                stat = tmp("stat", [NB, 5, BL, 6])
                mean_var = tmp("mv", [NB, 5, BL, 2])
                std = tmp("std", [NB, 5, BL])
                y_t = tmp("y_t", [D, 2, GN])
                turned_s = tmp("turned_s", [D1, 2, GN])
                ring_p, back_p = (RING1, BACK1) if last else (RING2, BACK2)
                p_proj = ps("p_proj", [D, max(ring_p) + 1, 512])
                p_y = ps("p_y", [NB, 2, 512])
                p_turn = ps("p_turn", [D, 2, 512])
                if last:
                    stat2 = tmp("stat2", [NB, 5, BL, 6])
                    mean_var2 = tmp("mv2", [NB, 5, BL, 2])
                    std2 = tmp("std2", [NB, 5, BL])
                    shift = tmp("shift", [NB, 5, BL])
                    mid = edge_room[0:NB, :, 0:BL * D].rearrange("p k (b f) -> p k b f", f=D)
                    p_pre = ps("p_pre", [NB, 3, 512])
                x_ready, row_stored = slots(name + "x_ready"), slots(name + "stored")
                mid_stored = slots(name + "mid_stored")
                (proj_done, y_t_done, y_done, stat_done, var_done, std_done, rstd_done, row_done,
                 row_free, turned, feat_done) = names(
                    *(name + n for n in ("proj_done", "y_t_done", "y_done", "stat_done", "var_done",
                                         "std_done", "rstd_done", "row_done", "row_free", "turned",
                                         "feat_done")))
                (mid_done, mid_free, stat2_done, var2_done, std2_done, rstd2_done,
                 norm_done, turned_kept, pre_done, pre_kept, ones_set) = names(
                    *(name + n for n in ("mid_done", "mid_free", "stat2_done", "var2_done",
                                         "std2_done", "rstd2_done", "norm_done",
                                         "turned_kept", "pre_done", "pre_kept", "ones_set")))
                y_used = mid_done if last else row_done
                block = own.enter_context(nc.Block())

                def pre_rows(k):
                    return got[0:NB, k, :].rearrange("p (b f) -> p b f", f=2 * D)

                @block.sync
                def _(sp):
                    sp.sem_inc(row_free, CREDIT)
                    sp.sem_inc(mid_free, CREDIT)

                    def load(g, k, count, body):
                        sp.wait_ge(mid_done, free_at(count, BACK5[k]))
                        sp.dma_start(xin[:, k, :, :], node_rows(x, g)).then_inc(x_ready[k], 16)

                    def store_mid(g, k, count, body):
                        sp.wait_ge(mid_done, done_at(count))
                        sp.dma_start(node_rows(x_mid, g), mid[:, k, :, :]).then_inc(mid_stored[k], 16)

                    def mid_is_stored(g, k, count, body):
                        sp.wait_ge(mid_stored[k], body * 16 + 16)
                        sp.sem_inc(mid_free, 1)

                    def store_x1(g, k, count, body):
                        sp.wait_ge(row_done, done_at(count))
                        sp.dma_start(node_rows(rows_x1, g), row[:, k, :, :]).then_inc(row_stored[k], 16)

                    def store_pre(g, k, count, body):
                        sp.wait_ge(pre_kept, done_at(count))
                        sp.dma_start(node_rows(rows_p, g), pre_rows(k)).then_inc(row_stored[k], 16)

                    def row_is_stored(g, k, count, body):
                        sp.wait_ge(row_stored[k], body * 16 + 16)
                        sp.sem_inc(row_free, 1)

                    if last:
                        skewed(sp, GBODIES, None, [(load, 0), (row_is_stored, 7), (mid_is_stored, 3),
                                                   (store_mid, 2), (store_pre, 6)])
                    else:
                        skewed(sp, GBODIES, None, [(store_x1, 0), (row_is_stored, 1)])

                @block.tensor
                def _(pe):
                    pe.sem_inc(y_done, CREDIT)
                    pe.sem_inc(turned, CREDIT)
                    pe.sem_inc(pre_done, CREDIT)

                    def project(g, k, count, body):
                        pe.wait_ge(y_t_done, free_at(count, back_p[k]))
                        to = p_proj[:, ring_p[k], 0:GN]
                        pe.matmul(to, wa[:, layer, :], columns(feat, D1, g), start=True, stop=False)
                        pe.matmul(to, wb[:, layer, :], columns(sums, D1, g), start=False, stop=True)\
                            .then_inc(proj_done, 1)

                    def to_rows(g, k, count, body):
                        pe.wait_ge(y_t_done, done_at(count))
                        pe.wait_ge(y_used, free_at(count, BACK2[k]))
                        for b in range(BL):
                            i = pe.transpose(p_y[:, RING2[k], b * D:(b + 1) * D],
                                             y_t[:, RING2[k], b * NB:(b + 1) * NB], ident[0:D, 0:D])
                        i.then_inc(y_done, 1)

                    def turn(g, k, count, body):
                        pe.wait_ge(row_done, done_at(count))
                        pe.wait_ge(feat_done, free_at(count, BACK2[k]))
                        for b in range(BL):
                            i = pe.transpose(p_turn[:, RING2[k], b * NB:(b + 1) * NB], row[:, k, b, :],
                                             ident[0:NB, 0:NB])
                        i.then_inc(turned, 1)

                    def table(g, k, count, body):
                        pe.wait_ge(turned_kept, count + 1)
                        pe.wait_ge(pre_kept, free_at(count, 1))
                        for b in range(BL):
                            i = pe.matmul(p_pre[:, b // 2, b % 2 * 2 * D:(b % 2 + 1) * 2 * D],
                                          turned_s[:, RING2[k], b * NB:(b + 1) * NB], w_pre[:, :],
                                          start=True, stop=True)
                        i.then_inc(pre_done, 1)

                    if last:
                        pe.wait_ge(ones_set, 1)
                        hold(pe)
                        skewed(pe, GBODIES, None, [(to_rows, 1), (project, 0), (turn, 3), (table, 4)])
                    else:
                        skewed(pe, GBODIES, None, [(project, 0), (to_rows, 1), (turn, 2)])

                @block.scalar
                def _(act):
                    act.sem_inc(y_t_done, CREDIT)
                    act.sem_inc(std_done, CREDIT)
                    act.sem_inc(std2_done, CREDIT)
                    act.sem_inc(feat_done, CREDIT)
                    act.sem_inc(pre_kept, CREDIT)
                    if last:
                        act.sem_inc(row_done, CREDIT)

                    def copy_y(g, k, count, body):
                        act.wait_ge(proj_done, count + 1)
                        act.wait_ge(y_done, free_at(count, BACK2[k]))
                        act.activation(y_t[:, RING2[k], :], p_proj[:, ring_p[k], 0:GN], ACT.Copy)\
                            .then_inc(y_t_done, 1)

                    def root(g, k, count, body):
                        act.wait_ge(var_done, count + 1)
                        act.wait_ge(y_used, free_at(count, BACK5[k]))
                        act.activation(std[:, k, :], mean_var[:, k, :, 1], ACT.Sqrt,
                                       scale=D / (D - 1)).then_inc(std_done, 1)

                    def root2(g, k, count, body):
                        act.wait_ge(var2_done, count + 1)
                        act.wait_ge(norm_done, free_at(count, BACK5[k]))
                        act.activation(std2[:, k, :], mean_var2[:, k, :, 1], ACT.Sqrt,
                                       bias=eps_col[:, :]).then_inc(std2_done, 1)

                    def relu(g, k, count, body):
                        act.wait_ge(norm_done, done_at(count))
                        act.wait_ge(turned, free_at(count, BACK5[k]))
                        for b in range(BL):
                            i = act.activation(row[:, k, b, :], mid[:, k, b, :], ACT.Relu,
                                               scale=std2[:, k, b:b + 1], bias=shift[:, k, b:b + 1])
                        i.then_inc(row_done, 1)

                    def keep(g, k, count, body):
                        act.wait_ge(turned, done_at(count))
                        if last:
                            act.wait_ge(pre_done, free_at(count, BACK2[k]))
                            act.activation(turned_s[0:D, RING2[k], :], p_turn[:, RING2[k], 0:GN],
                                           ACT.Copy).then_inc(turned_kept, 1)
                        act.activation(columns(feat, D, g), p_turn[:, RING2[k], 0:GN], ACT.Copy)\
                            .then_inc(feat_done, 1)

                    def keep_pre(g, k, count, body):
                        act.wait_ge(pre_done, done_at(count))
                        act.wait_ge(row_free, free_at(count, BACK5[k]))
                        four = got[0:NB, k, 0:8 * D].rearrange("p (b f) -> p b f", b=2)
                        act.activation(four, p_pre[:, 0:2, 0:4 * D], ACT.Copy)
                        act.activation(got[0:NB, k, 8 * D:10 * D], p_pre[:, 2, 0:2 * D], ACT.Copy)\
                            .then_inc(pre_kept, 1)

                    if last:
                        skewed(act, GBODIES, None, [(root2, 2), (relu, 3), (root, 1), (keep, 4),
                                                    (keep_pre, 5), (copy_y, 0)])
                    else:
                        skewed(act, GBODIES, None, [(copy_y, 0), (root, 1), (keep, 2)])

                @block.vector
                def _(dve):
                    if last:
                        dve.sem_inc(mid_done, CREDIT)
                        dve.sem_inc(norm_done, CREDIT)
                        dve.memset(turned_s[D:D1, :, :], 1.0).then_inc(ones_set, 1)
                    else:
                        dve.sem_inc(row_done, CREDIT)

                    def statistics(g, k, count, body):
                        dve.wait_ge(y_done, done_at(count))
                        dve.wait_ge(std_done, free_at(count, BACK5[k]))
                        for b in range(BL):
                            dve.bn_stats(stat[:, k, b, :], p_y[:, RING2[k], b * D:(b + 1) * D])\
                                .then_inc(stat_done, 1)
                        dve.wait_ge(stat_done, count * BL + BL)
                        hold(dve)
                        for b in range(BL):
                            i = dve.bn_aggr(mean_var[:, k, b, :], stat[:, k, b, :])
                        i.then_inc(var_done, 1)

                    def y_rows(k):
                        return p_y[:, RING2[k], 0:BL * D].rearrange("p (b f) -> p b f", f=D)

                    def scale(g, k, count, body):
                        dve.wait_ge(std_done, done_at(count))
                        dve.reciprocal(std[:, k, :], std[:, k, :]).then_inc(rstd_done, 1)
                        dve.wait_ge(row_free, free_at(count, BACK5[k]))
                        dve.wait_ge(turned, free_at(count, BACK5[k]))
                        dve.wait_ge(rstd_done, count + 1)
                        dve.tensor_tensor(row[:, k, :, :], y_rows(k), over(std[:, k, :]), ALU.mult)\
                            .then_inc(row_done, 1)

                    def residual(g, k, count, body):
                        dve.wait_ge(std_done, done_at(count))
                        dve.reciprocal(std[:, k, :], std[:, k, :]).then_inc(rstd_done, 1)
                        dve.wait_ge(mid_free, free_at(count, BACK5[k]))
                        dve.wait_ge(row_done, free_at(count, BACK5[k]))
                        dve.wait_ge(x_ready[k], body * 16 + 16)
                        dve.wait_ge(rstd_done, count + 1)
                        hold(dve)
                        for b in range(BL):
                            i = dve.scalar_tensor_tensor(
                                out=mid[:, k, b, :], in0=y_rows(k)[:, b, :], scalar=std[:, k, b:b + 1],
                                in1=xin[:, k, b, :], op0=ALU.mult, op1=ALU.add)
                        i.then_inc(mid_done, 1)
                        dve.wait_ge(std2_done, free_at(count, BACK5[k]))
                        dve.wait_ge(mid_done, done_at(count))
                        for b in range(BL):
                            dve.bn_stats(stat2[:, k, b, :], mid[:, k, b, :]).then_inc(stat2_done, 1)
                        dve.wait_ge(stat2_done, count * BL + BL)
                        hold(dve)
                        for b in range(BL):
                            i = dve.bn_aggr(mean_var2[:, k, b, :], stat2[:, k, b, :])
                        i.then_inc(var2_done, 1)

                    def normalise(g, k, count, body):
                        dve.wait_ge(std2_done, done_at(count))
                        dve.reciprocal(std2[:, k, :], std2[:, k, :]).then_inc(rstd2_done, 1)
                        dve.wait_ge(rstd2_done, count + 1)
                        dve.wait_ge(row_done, free_at(count, BACK5[k]))
                        dve.scalar_tensor_tensor(out=shift[:, k, :], in0=mean_var2[:, k, :, 0],
                                                 scalar=-1.0, in1=std2[:, k, :], op0=ALU.mult,
                                                 op1=ALU.mult).then_inc(norm_done, 1)

                    if last:
                        skewed(dve, GBODIES, None, [(normalise, 2), (residual, 1), (statistics, 0)])
                    else:
                        skewed(dve, GBODIES, None, [(scale, 1), (statistics, 0)])

        def node_update():
            with ExitStack() as own:
                names, slots = semaphores(own)

                def tmp(n, shape):
                    return own.enter_context(nc.sbuf_tensor("n3_" + n, shape, F32))

                def ps(n, shape):
                    return own.enter_context(nc.psum_tensor("n3_" + n, shape, F32))

                hidden = tmp("hidden", [D, 2, GN])
                upd = tmp("upd", [D, 2, GN])
                stat = tmp("stat", [NB, 5, BL, 6])
                mean_var = tmp("mv", [NB, 5, BL, 2])
                std = tmp("std", [NB, 5, BL])
                cent = spare
                p_hidden = ps("p_hidden", [D, 2, 512])
                p_upd = ps("p_upd", [D, 2, 512])
                p_y = ps("p_y", [NB, 2, 512])
                x_ready, out_stored = slots("n3_x_ready"), slots("n3_out_stored")
                (up_done, gelu_done, down_done, upd_done, y_done, stat_done, var_done, std_done,
                 rstd_done, cent_done, base_done, out_done, out_free) = names(
                    *("n3_" + n for n in ("up_done", "gelu_done", "down_done", "upd_done", "y_done",
                                          "stat_done", "var_done", "std_done", "rstd_done",
                                          "cent_done", "base_done", "out_done", "out_free")))
                block = own.enter_context(nc.Block())

                @block.gpsimd
                def _(pool):
                    def base(g, k, count, body):
                        pool.wait_ge(x_ready[k], body * 16 + 16)
                        pool.tensor_tensor(xin[:, k, :, :], xin[:, k, :, :],
                                           lnb_row[:, :].unsqueeze(1).broadcast_to([NB, BL, D]),
                                           ALU.add).then_inc(base_done, 1)

                    skewed(pool, GBODIES, None, [(base, 0)])

                @block.sync
                def _(sp):
                    sp.sem_inc(out_free, CREDIT)

                    def load(g, k, count, body):
                        sp.wait_ge(out_done, free_at(count, BACK5[k]))
                        sp.dma_start(xin[:, k, :, :], node_rows(x_mid, g)).then_inc(x_ready[k], 16)

                    def store(g, k, count, body):
                        sp.wait_ge(out_done, done_at(count))
                        sp.dma_start(node_rows(out, g), row[:, k, :, :]).then_inc(out_stored[k], 16)

                    def stored(g, k, count, body):
                        sp.wait_ge(out_stored[k], body * 16 + 16)
                        sp.sem_inc(out_free, 1)

                    skewed(sp, GBODIES, None, [(load, 0), (store, 3), (stored, 4)])

                @block.tensor
                def _(pe):
                    pe.sem_inc(down_done, CREDIT)
                    pe.sem_inc(y_done, CREDIT)

                    def up(g, k, count, body):
                        pe.wait_ge(gelu_done, free_at(count, BACK2[k]))
                        to = p_hidden[:, RING2[k], 0:GN]
                        pe.matmul(to, wu_self[:, :], columns(feat, D1, g), start=True, stop=False)
                        pe.matmul(to, wu_sum[:, :], columns(sums, D1, g), start=False, stop=True)\
                            .then_inc(up_done, 1)

                    def down(g, k, count, body):
                        pe.wait_ge(gelu_done, done_at(count))
                        pe.wait_ge(upd_done, free_at(count, BACK2[k]))
                        to = p_upd[:, RING2[k], 0:GN]
                        pe.matmul(to, uw2[:, :], hidden[:, RING2[k], :], start=True, stop=False)
                        pe.matmul(to, ident[0:D, 0:D], columns(feat, D, g), start=False, stop=True)\
                            .then_inc(down_done, 1)

                    def to_rows(g, k, count, body):
                        pe.wait_ge(upd_done, done_at(count))
                        pe.wait_ge(cent_done, free_at(count, BACK2[k]))
                        for b in range(BL):
                            i = pe.transpose(p_y[:, RING2[k], b * D:(b + 1) * D],
                                             upd[:, RING2[k], b * NB:(b + 1) * NB], ident[0:D, 0:D])
                        i.then_inc(y_done, 1)

                    skewed(pe, GBODIES, None, [(up, 0), (down, 1), (to_rows, 2)])

                @block.scalar
                def _(act):
                    act.sem_inc(gelu_done, CREDIT)
                    act.sem_inc(upd_done, CREDIT)
                    act.sem_inc(std_done, CREDIT)

                    def gelu(g, k, count, body):
                        act.wait_ge(up_done, count + 1)
                        act.wait_ge(down_done, free_at(count, BACK2[k]))
                        act.activation(hidden[:, RING2[k], :], p_hidden[:, RING2[k], 0:GN], ACT.Gelu)\
                            .then_inc(gelu_done, 1)

                    def copy_upd(g, k, count, body):
                        act.wait_ge(down_done, done_at(count))
                        act.wait_ge(y_done, free_at(count, BACK2[k]))
                        act.activation(upd[:, RING2[k], :], p_upd[:, RING2[k], 0:GN], ACT.Identity,
                                       bias=ub2_col[:, :]).then_inc(upd_done, 1)

                    def root(g, k, count, body):
                        act.wait_ge(var_done, count + 1)
                        act.wait_ge(out_done, free_at(count, BACK5[k]))
                        act.activation(std[:, k, :], mean_var[:, k, :, 1], ACT.Sqrt,
                                       bias=eps_col[:, :]).then_inc(std_done, 1)

                    skewed(act, GBODIES, None, [(gelu, 0), (copy_upd, 1), (root, 3)])

                @block.vector
                def _(dve):
                    dve.sem_inc(cent_done, CREDIT)
                    dve.sem_inc(out_done, CREDIT)

                    def centre(g, k, count, body):
                        dve.wait_ge(y_done, done_at(count))
                        dve.wait_ge(std_done, free_at(count, BACK5[k]))
                        for b in range(BL):
                            dve.bn_stats(stat[:, k, b, :], p_y[:, RING2[k], b * D:(b + 1) * D])\
                                .then_inc(stat_done, 1)
                        dve.wait_ge(stat_done, count * BL + BL)
                        hold(dve)
                        for b in range(BL):
                            i = dve.bn_aggr(mean_var[:, k, b, :], stat[:, k, b, :])
                        i.then_inc(var_done, 1)
                        dve.wait_ge(var_done, count + 1)
                        hold(dve)
                        for b in range(BL):
                            i = dve.scalar_tensor_tensor(
                                out=cent[:, k, b, :], in0=p_y[:, RING2[k], b * D:(b + 1) * D],
                                scalar=mean_var[:, k, b, 0:1], in1=lng_row[:, :],
                                op0=ALU.subtract, op1=ALU.mult)
                        i.then_inc(cent_done, 1)

                    def finish(g, k, count, body):
                        dve.wait_ge(std_done, done_at(count))
                        dve.reciprocal(std[:, k, :], std[:, k, :]).then_inc(rstd_done, 1)
                        dve.wait_ge(rstd_done, count + 1)
                        dve.wait_ge(cent_done, done_at(count))
                        dve.wait_ge(base_done, count + 1)
                        dve.wait_ge(out_free, free_at(count, BACK5[k]))
                        hold(dve)
                        for b in range(BL):
                            i = dve.scalar_tensor_tensor(
                                out=row[:, k, b, :], in0=cent[:, k, b, :], scalar=std[:, k, b:b + 1],
                                in1=xin[:, k, b, :], op0=ALU.mult, op1=ALU.add)
                        i.then_inc(out_done, 1)

                    skewed(dve, GBODIES, None, [(centre, 0), (finish, 2)])

        node_norm_first()
        linear_pass("l0", rows_h)
        node_layer("n1_", 0, False)
        linear_pass("l1", rows_x1)
        node_layer("n2_", 1, True)
        gated_pass("g", rows_p)
        node_update()


def kernel(**inputs):
    import numpy as np
    import concourse.bacc as bacc
    from concourse.bass_utils import run_bass_kernel_spmd

    a = {name: np.asarray(value) for name, value in inputs.items()}
    g = {name[len("L1_gnn_"):]: value for name, value in a.items() if name.startswith("L1_gnn_")}
    l = {name[len("L0_gnn_"):]: value for name, value in a.items() if name.startswith("L0_gnn_")}
    laid = {
        "x": a["x"],
        "src": a["src"].reshape(CHUNKS, TILES, P).transpose(0, 2, 1),
        "dst_tiles": a["dst"].reshape(CHUNKS * TILES, P).T,
        "dst_rows": a["dst"].reshape(BODIES, UNROLL, CE),
        "edge_t": a["edge_attr_32"].T,
        "W0T": l["W0"].transpose(0, 2, 1), "b0": l["b0"].reshape(2, D, 1),
        "W1T": l["W1"].transpose(0, 2, 1), "b1": l["b1"].reshape(2, D, 1),
        "W2": l["W2"], "b2": l["b2"].reshape(2, 1, D),
        "mW1": g["mW1"], "mb1": g["mb1"].reshape(1, D), "mW2T": g["mW2"].T, "mb2": g["mb2"].reshape(D, 1),
        "gW1": g["gW1"], "gb1": g["gb1"].reshape(1, D), "gW2": g["gW2"].reshape(D), "gb2": g["gb2"],
        "uW1": g["uW1"], "ub1": g["ub1"].reshape(1, D), "uW2": g["uW2"], "ub2": g["ub2"].reshape(D, 1),
        "ln_g": g["ln_g"], "ln_b": g["ln_b"],
    }
    nc = bacc.Bacc("TRN2", target_bir_lowering=False, num_devices=1)
    arrays, args = {}, []
    for name, value in laid.items():
        value = np.ascontiguousarray(value)
        arrays[f"in_{name}"] = value
        args.append(nc.dram_tensor(f"in_{name}", value.shape, mybir.dt.from_np(value.dtype),
                                   kind="ExternalInput").ap())
    args.append(nc.dram_tensor("out", (N, D), F32, kind="ExternalOutput").ap())
    for name, shape in (("rows_h", (N, D)), ("rows_x1", (N, D)), ("rows_p", (N, 2 * D)),
                        ("x_mid", (N, D)), ("extents", (2, BODIES, UNROLL))):
        args.append(nc.dram_tensor(name, shape, F32, kind="Internal").ap())
    gnn(nc, *args)
    r = run_bass_kernel_spmd(nc, [arrays], core_ids=[0])
    return r.results[0]["out"]
```

```python
import concourse.bass as bass
from concourse import mybir
from contextlib import ExitStack

F32 = mybir.dt.float32
I32 = mybir.dt.int32
ALU = mybir.AluOpType
ACT = mybir.ActivationFunctionType
AX = mybir.AxisListType

N, E, D, ED = 12500, 400000, 96, 32
D1 = D + 1
P = 128
EPS = 1e-5

UNROLL = 5
TILES = 5
CE = TILES * P
CHUNKS = E // CE
BODIES = CHUNKS // UNROLL
WIN_BITS = 5
WIN = 1 << WIN_BITS
ROUNDS_MAX = (N - 1) // WIN + 1
SCRATCH = N + WIN

NB = 100
BL = 5
GN = NB * BL
GROUPS = N // GN
GBODIES = GROUPS // UNROLL
assert BODIES * NB == N
assert CHUNKS * CE == E and BODIES * UNROLL == CHUNKS and GBODIES * UNROLL * GN == N

RING5, BACK5 = [0, 1, 2, 3, 4], [5, 5, 5, 5, 5]
RING2, BACK2 = [0, 1, 0, 1, 0], [1, 3, 2, 2, 2]
CREDIT = 5


def free_at(count, back):
    return count + (CREDIT + 1 - back)


def done_at(count):
    return count + (CREDIT + 1)


def skewed(eng, bodies, before, stages, blocks=(), blocks_before=None):
    most = max(skew for _, skew in [*stages, *blocks])
    peeled = max(1, -(-most // UNROLL))

    def place(first, k, skew):
        back = -(-max(skew - k, 0) // UNROLL)
        return (first - back if back else first), k - skew + UNROLL * back

    def emit(first, k, wanted):
        for stage, skew in blocks:
            j, kk = place(first, k, skew)
            if wanted(skew) and kk == 0 and not (isinstance(j, int) and j == bodies - 1):
                stage(j, j + blocks_before)
        for stage, skew in stages:
            if wanted(skew):
                body, kk = place(first, k, skew)
                total = body + before if before is not None else body
                stage(body * UNROLL + kk, kk, total * UNROLL + kk, total)

    for item in range(peeled * UNROLL):
        emit(item // UNROLL, item % UNROLL, lambda skew: item >= skew)
    with eng.Fori(peeled, bodies) as b:
        for k in range(UNROLL):
            emit(b, k, lambda skew: True)
    for item in range(most):
        emit(bodies + item // UNROLL, item % UNROLL, lambda skew: item < skew)


def gnn(nc, x, src, dst_tiles, dst_rows, edge_t, W0T, b0, W1T, b1, W2, b2, mW1, mb1, mW2T, mb2,
        gW1, gb1, gW2, gb2, uW1, ub1, uW2, ub2, ln_g, ln_b, out,
        rows_h, rows_x1, rows_p, x_mid, extents):
    ctx = ExitStack()
    with ctx:
        def sb(name, shape, dt=F32):
            return ctx.enter_context(nc.sbuf_tensor(name, shape, dt))

        feat = sb("feat", [D1, SCRATCH + NB])
        sums = sb("sums", [P, SCRATCH + NB])
        dst_rel = sb("dst_rel", [P, CHUNKS * TILES])
        start0 = sb("start0", [1, CHUNKS])
        start_f = sb("start_f", [1, CHUNKS])
        start_i = sb("start_i", [1, CHUNKS], I32)
        rounds_i = sb("rounds_i", [P, 1], I32)
        rounds_w = sb("rounds_w", [P, 1])
        block_at = sb("block_at", [1, BODIES], I32)
        first_left = sb("first_left", [P, 1], I32)
        left_base = sb("left_base", [P, 1], I32)
        ident = sb("ident", [P, P])
        window = sb("window", [P, WIN])
        wa = sb("wa", [D1, 2, D])
        wb = sb("wb", [D1, 2, D])
        w_pre = sb("w_pre", [D1, 2 * D])
        w_edge = sb("w_edge", [ED, 2 * D])
        wu_self = sb("wu_self", [D1, D])
        wu_sum = sb("wu_sum", [D1, D])
        uw2 = sb("uw2", [D, D])
        ident_b = sb("ident_b", [D1, D])
        gw2_row = sb("gw2_row", [P, D])
        gb2_half = sb("gb2_half", [P, 1])
        lng_row = sb("lng_row", [NB, D])
        lnb_row = sb("lnb_row", [NB, D])
        eps_col = sb("eps_col", [NB, 1])
        idx = sb("idx", [P, 5, TILES], I32)
        got = sb("got", [P, 5, TILES * 2 * D])
        hot = sb("hot", [P, 5, TILES, WIN])
        msg = sb("msg", [P, 5, TILES, D1])
        edge = sb("edge", [ED, 5, CE])
        zz = sb("zz", [P, 5, TILES])
        gate = sb("gate", [P, 5, TILES])

        def semaphores(own):
            used = []

            def name(n):
                used.append(nc.alloc_semaphore(name=n))
                return used[-1]

            def clear():
                nc.clear_and_free_semaphores(used)
                nc.all_engine_barrier()

            own.callback(clear)
            return (lambda *list_: [name(n) for n in list_]), (lambda n: [name(f"{n}{k}") for k in range(5)])

        passed = ctx.enter_context(nc.semaphore("passed"))

        def hold(eng):
            eng.sem_inc(passed, 1)

        def node_rows(table, g):
            return table[bass.ds(g * GN, GN), :].rearrange("(b p) f -> p b f", p=NB)

        def columns(t, rows, g):
            return t[0:rows, bass.ds(g * GN, GN)]

        def node_norm_first():
            with ExitStack() as own:
                names, slots = semaphores(own)

                def ps(name, shape):
                    return own.enter_context(nc.psum_tensor(name, shape, F32))

                def tmp(name, shape, dt=F32):
                    return own.enter_context(nc.sbuf_tensor(name, shape, dt))

                w0t = tmp("w0t", [D, 2, D1])
                w1t = tmp("w1t", [D, 2, D1])
                mw2t = tmp("mw2t", [D, D1])
                w2a = tmp("w2a", [D, 2, D])
                w2b = tmp("w2b", [D, 2, D])
                uw1b = tmp("uw1b", [D, D])
                b2r = tmp("b2r", [1, 2, D])
                last_row = tmp("last_row", [1, D1])
                lo = tmp("lo", [BODIES, UNROLL])
                hi = tmp("hi", [BODIES, UNROLL])
                starts = tmp("starts", [P, CHUNKS])
                window_i = tmp("window_i", [P, WIN], I32)
                widest = tmp("widest", [P, 10])
                widest_i = tmp("widest_i", [P, 2], I32)
                dst_i = got[:, :, :].rearrange("p a b -> p (a b)")[:, 0:CHUNKS * TILES].bitcast(I32)
                dst_c = sums[0:BODIES, 0:UNROLL * CE].bitcast(I32).rearrange("p (u e) -> p u e", u=UNROLL)
                his = tmp("his", [P, CHUNKS])[:, :]
                nodes_i = tmp("nodes_i", [P, BODIES], I32)
                nodes_f = tmp("nodes_f", [P, BODIES])
                ahead = tmp("ahead", [P, CHUNKS])
                xin = tmp("n0_xin", [NB, 5, BL, D])
                row = tmp("n0_row", [NB, 5, BL, D])
                stat = tmp("n0_stat", [NB, 5, BL, 6])
                mean_var = tmp("n0_mv", [NB, 5, BL, 2])
                std = tmp("n0_std", [NB, 5, BL])
                shift = tmp("n0_shift", [NB, 5, BL])
                p_w = ps("p_w", [D1, 5, 512])
                p_t = ps("n0_pt", [D, 2, 512])
                (w_in, halved, w_mul, w_out, dst_in, tiles_in, iota_done, sel_set, ext_out, ext_in,
                 min_done, wide, rel_done, consts, ones_done, nodes_done) = names(
                    "w_in", "halved", "w_mul", "w_out", "dst_in", "tiles_in", "iota_done", "sel_set",
                    "ext_out", "ext_in", "min_done", "wide", "rel_done", "consts",
                    "ones_done", "nodes_done")
                x_ready, row_stored = slots("n0_x_ready"), slots("n0_stored")
                (stat_done, var_done, std_done, rstd_done, norm_done, row_done, turned, row_free,
                 feat_done) = names(*("n0_" + n for n in (
                     "stat_done", "var_done", "std_done", "rstd_done", "norm_done", "row_done",
                     "turned", "row_free", "feat_done")))
                loads = [(w_pre[0:D, 0:D], mW1[0:D, :]), (w_pre[0:D, D:2 * D], gW1[0:D, :]),
                         (w_pre[D:D1, 0:D], mb1), (w_pre[D:D1, D:2 * D], gb1),
                         (w_edge[:, 0:D], mW1[D:D + ED, :]), (w_edge[:, D:2 * D], gW1[D:D + ED, :]),
                         (wu_self[0:D, :], uW1[0:D, :]), (wu_self[D:D1, :], ub1),
                         (uw1b[:, :], uW1[D:2 * D, :]), (uw2[:, :], uW2), (ident_b[D:D1, :], ub2),
                         (gw2_row[:, :], gW2.partition_broadcast(P)),
                         (gb2_half[:, :], gb2.partition_broadcast(P)),
                         (lng_row[:, :], ln_g.partition_broadcast(NB)),
                         (lnb_row[:, :], ln_b.partition_broadcast(NB)),
                         (mw2t[:, 0:D], mW2T), (mw2t[:, D:D1], mb2)]
                for i in range(2):
                    loads += [(w0t[:, i, 0:D], W0T[i]), (w0t[:, i, D:D1], b0[i]),
                              (w1t[:, i, 0:D], W1T[i]), (w1t[:, i, D:D1], b1[i]),
                              (w2a[:, i, :], W2[i, 0:D, :]), (w2b[:, i, :], W2[i, D:2 * D, :]),
                              (b2r[:, i, :], b2[i])]
                block = own.enter_context(nc.Block())

                @block.sync
                def _(sp):
                    sp.sem_inc(row_free, CREDIT)

                    def load(g, k, count, body):
                        sp.wait_ge(row_done, free_at(count, BACK5[k]))
                        sp.dma_start(xin[:, k, :, :], node_rows(x, g)).then_inc(x_ready[k], 16)

                    def store(g, k, count, body):
                        sp.wait_ge(row_done, done_at(count))
                        sp.dma_start(node_rows(rows_h, g), row[:, k, :, :]).then_inc(row_stored[k], 16)

                    def stored(g, k, count, body):
                        sp.wait_ge(row_stored[k], 16 * (body + 1))
                        sp.sem_inc(row_free, 1)

                    skewed(sp, GBODIES, None, [(load, 0), (store, 3), (stored, 4)])

                @block.gpsimd
                def _(pool):
                    pool.memset(ident[:, :], 0.0).then_inc(sel_set, 1)
                    pool.wait_ge(sel_set, 1)
                    pool.affine_select(out=ident[:, :], in_=ident[:, :], compare_op=ALU.not_equal,
                                       fill=1.0, base=0, pattern=[[-1, P]], channel_multiplier=1)\
                        .then_inc(sel_set, 1)
                    pool.iota(window_i[:, :], pattern=[[1, WIN]], base=0, channel_multiplier=0)\
                        .then_inc(iota_done, 1)
                    pool.iota(nodes_i[:, :], pattern=[[NB, BODIES]], base=0, channel_multiplier=0)\
                        .then_inc(nodes_done, 1)
                    pool.dma_start(dst_c, dst_rows).then_inc(dst_in, 16)
                    pool.dma_start(dst_i, dst_tiles).then_inc(tiles_in, 16)
                    pool.wait_ge(iota_done, 1)
                    pool.wait_ge(nodes_done, 1)
                    pool.memset(feat[D:D1, :], 1.0).then_inc(ones_done, 1)
                    pool.wait_ge(min_done, 2)
                    pool.dma_start(extents[0], lo[:, :]).then_inc(ext_out, 16)
                    pool.dma_start(extents[1], hi[:, :]).then_inc(ext_out, 16)
                    pool.wait_ge(ext_out, 32)
                    flat = extents.rearrange("a b u -> a (b u)")
                    pool.dma_start(starts[:, :], flat[0:1, :].partition_broadcast(P)).then_inc(ext_in, 16)
                    pool.dma_start(his, flat[1:2, :].partition_broadcast(P)).then_inc(ext_in, 16)
                    pool.wait_ge(ext_in, 32)
                    pool.wait_ge(ones_done, 1)

                @block.vector
                def _(dve):
                    dve.memset(last_row[:, :], 0.0).then_inc(consts, 1)
                    dve.memset(msg[:, :, :, D:D1], 1.0).then_inc(consts, 1)
                    dve.memset(eps_col[:, :], EPS).then_inc(consts, 1)
                    dve.wait_ge(consts, 3)
                    dve.memset(last_row[:, D:D1], 1.0).then_inc(consts, 1)
                    dve.wait_ge(sel_set, 2)
                    dve.tensor_copy(ident_b[0:D, :], ident[0:D, 0:D]).then_inc(consts, 1)
                    dve.wait_ge(consts, 5)
                    dve.wait_ge(iota_done, 1)
                    dve.tensor_copy(window[:, :], window_i[:, :]).then_inc(iota_done, 1)
                    dve.wait_ge(nodes_done, 1)
                    dve.tensor_copy(nodes_f[:, :], nodes_i[:, :]).then_inc(nodes_done, 1)
                    dve.memset(feat[0:D, SCRATCH:SCRATCH + NB], 1.0).then_inc(iota_done, 1)
                    dve.wait_ge(iota_done, 3)
                    dve.wait_ge(nodes_done, 2)
                    dve.wait_ge(dst_in, 16)
                    dve.tensor_reduce(lo[:, :], dst_c, AX.X, ALU.min).then_inc(min_done, 1)
                    dve.tensor_reduce(hi[:, :], dst_c, AX.X, ALU.max).then_inc(min_done, 1)
                    dve.sem_inc(norm_done, CREDIT)
                    dve.sem_inc(feat_done, CREDIT)

                    def statistics(g, k, count, body):
                        dve.wait_ge(x_ready[k], 16 * (body + 1))
                        dve.wait_ge(std_done, free_at(count, BACK5[k]))
                        for b in range(BL):
                            dve.bn_stats(stat[:, k, b, :], xin[:, k, b, :]).then_inc(stat_done, 1)

                    def aggregate(g, k, count, body):
                        dve.wait_ge(stat_done, count * BL + BL)
                        hold(dve)
                        for b in range(BL):
                            i = dve.bn_aggr(mean_var[:, k, b, :], stat[:, k, b, :])
                        i.then_inc(var_done, 1)

                    def shifts(g, k, count, body):
                        dve.wait_ge(std_done, done_at(count))
                        dve.reciprocal(std[:, k, :], std[:, k, :]).then_inc(rstd_done, 1)
                        dve.wait_ge(rstd_done, count + 1)
                        dve.wait_ge(row_done, free_at(count, BACK5[k]))
                        dve.scalar_tensor_tensor(out=shift[:, k, :], in0=mean_var[:, k, :, 0],
                                                 scalar=-1.0, in1=std[:, k, :], op0=ALU.mult,
                                                 op1=ALU.mult).then_inc(norm_done, 1)

                    def keep(g, k, count, body):
                        dve.wait_ge(turned, count + 1)
                        dve.tensor_copy(columns(feat, D, g), p_t[:, RING2[k], 0:GN])\
                            .then_inc(feat_done, 1)

                    skewed(dve, GBODIES, None, [(statistics, 0), (keep, 3), (aggregate, 0), (shifts, 1)])
                    dve.wait_ge(ext_in, 32)
                    dve.tensor_tensor(his, his, starts[:, :], ALU.subtract).then_inc(wide, 1)
                    dve.tensor_copy(start0[:, :], starts[0:1, :]).then_inc(wide, 1)
                    dve.tensor_copy(start_f[:, :], starts[0:1, :]).then_inc(wide, 1)
                    dve.tensor_copy(start_i[:, :], starts[0:1, :]).then_inc(wide, 1)
                    dve.wait_ge(wide, 4)
                    dve.tensor_reduce(widest[:, 0:1], his, AX.X, ALU.max).then_inc(wide, 1)
                    dve.wait_ge(wide, 5)
                    dve.tensor_copy(widest_i[:, 0:1], widest[:, 0:1]).then_inc(wide, 1)
                    dve.wait_ge(wide, 6)
                    dve.tensor_scalar(widest_i[:, 1:2], widest_i[:, 0:1], WIN_BITS, None,
                                      ALU.arith_shift_right).then_inc(wide, 1)
                    dve.wait_ge(wide, 7)
                    dve.tensor_scalar(widest[:, 1:2], widest_i[:, 1:2], 1.0, None, ALU.add).then_inc(wide, 1)
                    dve.wait_ge(wide, 8)
                    dve.tensor_copy(rounds_i[:, :], widest[:, 1:2]).then_inc(wide, 1)
                    dve.tensor_scalar(rounds_w[:, :], widest[:, 1:2], float(WIN), None, ALU.mult)\
                        .then_inc(wide, 1)
                    dve.tensor_tensor(ahead[:, :].rearrange("p (b u) -> p b u", u=UNROLL),
                                      starts[:, :].rearrange("p (b u) -> p b u", u=UNROLL),
                                      nodes_f[:, :].unsqueeze(2).broadcast_to([P, BODIES, UNROLL]),
                                      ALU.subtract).then_inc(wide, 1)
                    dve.wait_ge(wide, 11)
                    dve.tensor_reduce(widest[:, 2:3], ahead[:, :], AX.X, ALU.min).then_inc(wide, 1)
                    dve.wait_ge(wide, 12)
                    dve.tensor_scalar(widest[:, 3:4], widest[:, 2:3], float(-NB), None, ALU.is_ge)\
                        .then_inc(wide, 1)
                    dve.tensor_scalar(widest[:, 4:5], widest[:, 1:2], 1.0, None, ALU.is_le).then_inc(wide, 1)
                    dve.wait_ge(wide, 14)
                    dve.tensor_tensor(widest[:, 5:6], widest[:, 3:4], widest[:, 4:5], ALU.mult)\
                        .then_inc(wide, 1)
                    dve.wait_ge(wide, 15)
                    dve.tensor_scalar(widest[:, 7:8], widest[:, 5:6], float(BODIES - 1), None, ALU.mult)\
                        .then_inc(wide, 1)
                    dve.tensor_scalar(widest[:, 8:9], widest[:, 1:2], float(BODIES - 1), None, ALU.mult)\
                        .then_inc(wide, 1)
                    dve.tensor_scalar(widest[:, 6:7], widest[:, 5:6], float(-SCRATCH), float(SCRATCH),
                                      ALU.mult, ALU.add).then_inc(wide, 1)
                    dve.wait_ge(wide, 18)
                    dve.tensor_tensor(widest[:, 9:10], widest[:, 8:9], widest[:, 7:8], ALU.subtract)\
                        .then_inc(wide, 1)
                    dve.tensor_copy(first_left[:, :], widest[:, 7:8]).then_inc(wide, 1)
                    dve.tensor_scalar(nodes_f[:, :], nodes_f[:, :], widest[:, 6:7], None, ALU.max)\
                        .then_inc(wide, 1)
                    dve.wait_ge(wide, 21)
                    dve.tensor_copy(left_base[:, :], widest[:, 9:10]).then_inc(wide, 1)
                    dve.tensor_copy(block_at[:, :], nodes_f[0:1, :]).then_inc(wide, 1)
                    dve.wait_ge(wide, 23)
                    dve.wait_ge(tiles_in, 16)
                    dve.tensor_tensor(dst_rel[:, :].rearrange("p (c t) -> p c t", t=TILES),
                                      dst_i.rearrange("p (c t) -> p c t", t=TILES),
                                      starts[:, :].unsqueeze(2).broadcast_to([P, CHUNKS, TILES]),
                                      ALU.subtract).then_inc(rel_done, 1)
                    dve.wait_ge(rel_done, 1)

                @block.scalar
                def _(act):
                    for to, of in loads:
                        act.dma_start(to, of).then_inc(w_in, 16)
                    act.sem_inc(std_done, CREDIT)
                    act.sem_inc(row_done, CREDIT)
                    act.wait_ge(consts, 4)

                    def root(g, k, count, body):
                        act.wait_ge(var_done, count + 1)
                        act.wait_ge(norm_done, free_at(count, BACK5[k]))
                        act.activation(std[:, k, :], mean_var[:, k, :, 1], ACT.Sqrt,
                                       bias=eps_col[:, :]).then_inc(std_done, 1)

                    def relu(g, k, count, body):
                        act.wait_ge(norm_done, done_at(count))
                        act.wait_ge(row_free, free_at(count, BACK5[k]))
                        for b in range(BL):
                            i = act.activation(row[:, k, b, :], xin[:, k, b, :], ACT.Relu,
                                               scale=std[:, k, b:b + 1], bias=shift[:, k, b:b + 1])
                        i.then_inc(row_done, 1)

                    skewed(act, GBODIES, None, [(root, 0), (relu, 1)])
                    act.wait_ge(w_in, 16 * len(loads))
                    act.mul(gb2_half[:, :], gb2_half[:, :], 0.5).then_inc(halved, 1)
                    act.wait_ge(w_mul, 1)
                    for n, to in enumerate((wa[:, 0, :], wa[:, 1, :], wb[:, 0, :], wb[:, 1, :], wu_sum[:, :])):
                        act.activation(to, p_w[:, n, 0:D], ACT.Copy).then_inc(w_out, 1)
                    act.wait_ge(w_out, 5)
                    act.wait_ge(halved, 1)

                @block.tensor
                def _(pe):
                    pe.wait_ge(sel_set, 2)

                    def turn(g, k, count, body):
                        pe.wait_ge(row_done, done_at(count))
                        pe.wait_ge(feat_done, free_at(count, BACK2[k]))
                        for b in range(BL):
                            i = pe.transpose(p_t[:, RING2[k], b * NB:(b + 1) * NB], row[:, k, b, :],
                                             ident[0:NB, 0:NB])
                        i.then_inc(turned, 1)

                    skewed(pe, GBODIES, None, [(turn, 0)])
                    pe.wait_ge(w_in, 16 * len(loads))
                    pe.wait_ge(consts, 4)
                    for i in range(2):
                        pe.matmul(p_w[:, i, 0:D], w1t[:, i, :], w2a[:, i, :], start=True, stop=False)
                        pe.matmul(p_w[:, i, 0:D], last_row[:, :], b2r[:, i, :], start=False, stop=True)
                        pe.matmul(p_w[:, 2 + i, 0:D], w0t[:, i, :], w2b[:, i, :], start=True, stop=True)
                    pe.matmul(p_w[:, 4, 0:D], mw2t[:, :], uw1b[:, :], start=True, stop=True).then_inc(w_mul, 1)

        def block_rows(table, j):
            return table[bass.ds(j * NB, NB), :]

        def rounds_of(eng):
            return eng.value_load(rounds_i[0:1, 0:1], min_val=1, max_val=ROUNDS_MAX)

        def left_blocks(eng, stages):
            left = eng.value_load(first_left[0:1, 0:1], min_val=0, max_val=BODIES - 1)
            base = eng.value_load(left_base[0:1, 0:1], min_val=0, max_val=ROUNDS_MAX * (BODIES - 1))
            with eng.Fori(left, BODIES) as j:
                for stage in stages:
                    stage(j, base + j)

        def in_place(stage):
            return lambda j, done: stage(j, done, j * NB)

        def columns_at(eng, reg, j):
            eng.reg_load(reg, block_at[0:1, bass.ds(j, 1)])
            return eng.snap(reg, min_val=0, max_val=SCRATCH)

        def load_index(sp, idx_ready, rows_used):
            def indices(chunk, k, count, body):
                sp.wait_ge(rows_used, free_at(count, BACK5[k]))
                sp.dma_start(idx[:, k, :], src[bass.ds(chunk, 1)].rearrange("c p t -> (c p) t"))\
                    .then_inc(idx_ready[k], 16)
            return indices

        def gathered_at(body):
            return body * (16 * TILES) + 16 * TILES

        def gather_rows(pool, table, width, pitch, idx_ready, gathered, free):
            rounds = rounds_of(pool)
            with pool.Fori(0, rounds) as r:
                with pool.Fori(0, BODIES) as b:
                    for k in range(UNROLL):
                        body = r * BODIES + b
                        pool.wait_ge(idx_ready[k], body * 16 + 16)
                        hold(pool)
                        pool.wait_ge(free, body * UNROLL + (k + 1))
                        hold(pool)
                        for t in range(TILES):
                            pool.indirect_dma_start(
                                got[:, k, t * pitch:t * pitch + width], None, table,
                                bass.IndirectOffsetOnAxis(idx[:, k, t:t + 1], axis=0))\
                                .then_inc(gathered[k], 16)

        def one_hot(dve, chunk, k):
            rel = dst_rel[:, bass.ds(chunk * TILES, TILES)].unsqueeze(2).broadcast_to([P, TILES, WIN])
            cols = window[:, :].unsqueeze(1).broadcast_to([P, TILES, WIN])
            return dve.tensor_tensor(hot[:, k, :, :], rel, cols, ALU.is_equal)

        def add_window(dve, chunk, p_seg_slot, start_reg):
            dve.reg_load(start_reg, start_i[0:1, bass.ds(chunk, 1)])
            start = dve.snap(start_reg, min_val=0, max_val=N)
            where = sums[0:D1, bass.ds(start, WIN)]
            return dve.tensor_tensor(where, where, p_seg_slot, ALU.add)

        def move_windows(dve, moved, r):
            dve.tensor_scalar(dst_rel[:, :], dst_rel[:, :], float(-WIN), None, ALU.add).then_inc(moved, 1)
            dve.tensor_scalar(start_f[:, :], start_f[:, :], float(WIN), None, ALU.add).then_inc(moved, 1)
            dve.wait_ge(moved, r * 3 + 2)
            dve.tensor_scalar(start_i[:, :], start_f[:, :], float(N), None, ALU.min).then_inc(moved, 1)
            dve.wait_ge(moved, r * 3 + 3)
            hold(dve)

        def restore_windows(dve, back):
            dve.tensor_scalar(dst_rel[:, :], dst_rel[:, :], rounds_w[:, 0:1], None, ALU.add).then_inc(back, 1)
            dve.tensor_copy(start_f[:, :], start0[:, :]).then_inc(back, 1)
            dve.tensor_copy(start_i[:, :], start0[:, :]).then_inc(back, 1)
            dve.wait_ge(back, 3)

        def linear_pass(name, layer, table, last):
            with ExitStack() as own:
                names, slots = semaphores(own)

                def tmp(n, shape):
                    return own.enter_context(nc.sbuf_tensor(name + n, shape, F32))

                p_seg = own.enter_context(nc.psum_tensor(name + "seg", [D1, 5, 512], F32))
                p_node = own.enter_context(nc.psum_tensor(name + "node", [P, 3, 512], F32))
                p_proj, p_y, p_turn = p_node[0:D, 0, 0:NB], p_node[0:NB, 1, 0:D], p_node[0:D, 2, 0:NB]
                p_pre = p_node[0:NB, 2, 256:256 + 2 * D]
                y_t = tmp("y_t", [D, NB])
                row = tmp("row", [NB, D])
                stat, mean_var, std = tmp("stat", [NB, 6]), tmp("mv", [NB, 2]), tmp("std", [NB, 1])
                if last:
                    x_row, mid, pre_row = tmp("x_row", [NB, D]), tmp("mid", [NB, D]), tmp("pre_row", [NB, 2 * D])
                    stat2, mean_var2 = tmp("stat2", [NB, 6]), tmp("mv2", [NB, 2])
                    std2, shift = tmp("std2", [NB, 1]), tmp("shift", [NB, 1])
                    turned_s = tmp("turned_s", [D1, NB])
                idx_ready, gathered = slots(name + "idx_ready"), slots(name + "gathered")
                (hot_done, seg_done, added, zeroed, moved, back, proj_done, y_t_done, y_done, stat_done,
                 var_done, std_done, rstd_done, row_done, row_stored, row_free, turned, feat_done) = names(
                    *(name + n for n in (
                        "hot_done", "seg_done", "added", "zeroed", "moved", "back", "proj_done",
                        "y_t_done", "y_done", "stat_done", "var_done", "std_done", "rstd_done",
                        "row_done", "row_stored", "row_free", "turned", "feat_done")))
                if last:
                    (x_ready, mid_done, mid_stored, mid_free, stat2_done, var2_done, std2_done,
                     rstd2_done, norm_done, turned_kept, pre_done, pre_kept, ones_set) = names(
                        *(name + n for n in (
                            "x_ready", "mid_done", "mid_stored", "mid_free", "stat2_done", "var2_done",
                            "std2_done", "rstd2_done", "norm_done", "turned_kept", "pre_done",
                            "pre_kept", "ones_set")))
                y_used = mid_done if last else row_done
                block = own.enter_context(nc.Block())

                def rows_of(k):
                    return got[:, k, 0:TILES * D1].rearrange("p (t f) -> p t f", f=D1)

                @block.sync
                def _(sp):
                    sp.sem_inc(row_free, CREDIT)
                    if last:
                        sp.sem_inc(mid_free, CREDIT)
                    rounds = rounds_of(sp)

                    def load(j, done):
                        sp.wait_ge(mid_done, free_at(done, 1))
                        sp.dma_start(x_row[:, :], block_rows(x, j)).then_inc(x_ready, 16)

                    def store_mid(j, done):
                        sp.wait_ge(mid_done, done_at(done))
                        sp.dma_start(block_rows(x_mid, j), mid[:, :]).then_inc(mid_stored, 16)

                    def mid_is_stored(j, done):
                        sp.wait_ge(mid_stored, done * 16 + 16)
                        sp.sem_inc(mid_free, 1)

                    def store_x1(j, done):
                        sp.wait_ge(row_done, done_at(done))
                        sp.dma_start(block_rows(rows_x1, j), row[:, :]).then_inc(row_stored, 16)

                    def store_pre(j, done):
                        sp.wait_ge(pre_kept, done_at(done))
                        sp.dma_start(block_rows(rows_p, j), pre_row[:, :]).then_inc(row_stored, 16)

                    def row_is_stored(j, done):
                        sp.wait_ge(row_stored, done * 16 + 16)
                        sp.sem_inc(row_free, 1)

                    if last:
                        blocks = [(load, 16), (store_mid, 20), (mid_is_stored, 21), (store_pre, 22),
                                  (row_is_stored, 23)]
                    else:
                        blocks = [(store_x1, 19), (row_is_stored, 20)]
                    with sp.Fori(0, rounds) as r:
                        skewed(sp, BODIES, r * BODIES, [(load_index(sp, idx_ready, seg_done), 0)],
                               blocks, r * (BODIES - 1))
                    left_blocks(sp, [stage for stage, _ in blocks])

                @block.gpsimd
                def _(pool):
                    gather_rows(pool, table, D, D1, idx_ready, gathered, seg_done)

                @block.tensor
                def _(pe):
                    pe.sem_inc(seg_done, CREDIT)
                    pe.sem_inc(y_done, CREDIT)
                    pe.sem_inc(turned, CREDIT)
                    if last:
                        pe.sem_inc(pre_done, CREDIT)
                        pe.wait_ge(ones_set, 1)
                        hold(pe)
                    rounds = rounds_of(pe)
                    at_reg = pe.alloc_register(name + "pe_at")
                    pe.wait_ge(zeroed, 1)
                    hold(pe)

                    def project(j, done, at):
                        pe.wait_ge(y_t_done, free_at(done, 1))
                        pe.wait_ge(feat_done, free_at(done, 1))
                        hold(pe)
                        pe.matmul(p_proj, wa[:, layer, :], feat[:, bass.ds(at, NB)], start=True, stop=False)
                        pe.matmul(p_proj, wb[:, layer, :], sums[0:D1, bass.ds(at, NB)], start=False,
                                  stop=True).then_inc(proj_done, 1)

                    def to_rows(j, done):
                        pe.wait_ge(y_t_done, done_at(done))
                        pe.wait_ge(y_used, free_at(done, 1))
                        pe.transpose(p_y, y_t[:, :], ident[0:D, 0:D]).then_inc(y_done, 1)

                    def turn(j, done):
                        pe.wait_ge(row_done, done_at(done))
                        pe.wait_ge(feat_done, free_at(done, 1))
                        if last:
                            pe.wait_ge(pre_kept, free_at(done, 1))
                        pe.transpose(p_turn, row[:, :], ident[0:NB, 0:NB]).then_inc(turned, 1)

                    def make_table(j, done):
                        pe.wait_ge(feat_done, done_at(done))
                        pe.wait_ge(turned_kept, done + 1)
                        pe.matmul(p_pre, turned_s[:, :], w_pre[:, :], start=True, stop=True)\
                            .then_inc(pre_done, 1)

                    with pe.Fori(0, rounds) as r:
                        def segment(chunk, k, count, body):
                            pe.wait_ge(gathered[k], gathered_at(body))
                            pe.wait_ge(hot_done, count + 1)
                            pe.wait_ge(added, free_at(count, BACK5[k]))
                            for t in range(TILES):
                                i = pe.matmul(p_seg[:, k, 0:WIN], rows_of(k)[:, t, :], hot[:, k, t, :],
                                              start=t == 0, stop=t == TILES - 1)
                            i.then_inc(seg_done, 1)

                        def project_within(j, done):
                            pe.wait_ge(added, (r * BODIES + j) * UNROLL + (2 * UNROLL + CREDIT))
                            hold(pe)
                            project(j, done, columns_at(pe, at_reg, j))

                        blocks = ([(make_table, 16)] if last else []) \
                            + [(turn, 15), (to_rows, 12), (project_within, 11)]
                        skewed(pe, BODIES, r * BODIES, [(segment, 0)], blocks, r * (BODIES - 1))
                    pe.wait_ge(added, rounds * CHUNKS + CREDIT)
                    hold(pe)
                    left_blocks(pe,
                                [in_place(project), to_rows, turn] + ([make_table] if last else []))

                @block.scalar
                def _(act):
                    act.sem_inc(y_t_done, CREDIT)
                    act.sem_inc(std_done, CREDIT)
                    act.sem_inc(feat_done, CREDIT)
                    if last:
                        act.sem_inc(std2_done, CREDIT)
                        act.sem_inc(pre_kept, CREDIT)
                        act.sem_inc(row_done, CREDIT)
                    rounds = rounds_of(act)
                    at_reg = act.alloc_register(name + "act_at")

                    def copy_y(j, done):
                        act.wait_ge(proj_done, done + 1)
                        act.wait_ge(y_done, free_at(done, 1))
                        act.activation(y_t[:, :], p_proj, ACT.Copy).then_inc(y_t_done, 1)

                    def root(j, done):
                        act.wait_ge(var_done, done + 1)
                        act.wait_ge(y_used, free_at(done, 1))
                        act.activation(std[:, :], mean_var[:, 1:2], ACT.Sqrt, scale=D / (D - 1))\
                            .then_inc(std_done, 1)

                    def root2(j, done):
                        act.wait_ge(var2_done, done + 1)
                        act.wait_ge(row_done, free_at(done, 1))
                        act.activation(std2[:, :], mean_var2[:, 1:2], ACT.Sqrt, bias=eps_col[:, :])\
                            .then_inc(std2_done, 1)

                    def relu(j, done):
                        act.wait_ge(norm_done, done_at(done))
                        act.wait_ge(turned, free_at(done, 1))
                        act.activation(row[:, :], mid[:, :], ACT.Relu, scale=std2[:, 0:1],
                                       bias=shift[:, 0:1]).then_inc(row_done, 1)

                    def keep(j, done, at):
                        act.wait_ge(turned, done_at(done))
                        if last:
                            act.wait_ge(pre_done, free_at(done, 1))
                            act.activation(turned_s[0:D, :], p_turn, ACT.Copy).then_inc(turned_kept, 1)
                        act.activation(feat[0:D, bass.ds(at, NB)], p_turn, ACT.Copy)\
                            .then_inc(feat_done, 1)

                    def keep_pre(j, done):
                        act.wait_ge(pre_done, done_at(done))
                        act.wait_ge(row_free, free_at(done, 1))
                        act.activation(pre_row[:, :], p_pre, ACT.Copy).then_inc(pre_kept, 1)

                    def keep_within(j, done):
                        keep(j, done, columns_at(act, at_reg, j))

                    def chain(kept):
                        return [copy_y, root, root2, relu, kept, keep_pre] if last else [copy_y, root, kept]

                    with act.Fori(0, rounds) as r:
                        with act.Fori(0, BODIES - 1) as b:
                            for stage in chain(keep_within):
                                stage(b, r * (BODIES - 1) + b)
                    left_blocks(act, chain(in_place(keep)))

                @block.vector
                def _(dve):
                    dve.sem_inc(added, CREDIT)
                    rounds = rounds_of(dve)
                    start_reg = dve.alloc_register(name + "start")
                    for k in range(5):
                        i = dve.memset(rows_of(k)[:, :, D:D1], 1.0)
                    i.then_inc(zeroed, 1)
                    dve.memset(sums[:, :], 0.0).then_inc(zeroed, 1)
                    if last:
                        dve.sem_inc(mid_done, CREDIT)
                        dve.sem_inc(norm_done, CREDIT)
                        dve.memset(turned_s[D:D1, :], 1.0).then_inc(ones_set, 1)
                    else:
                        dve.sem_inc(row_done, CREDIT)
                    dve.wait_ge(zeroed, 2)
                    hold(dve)

                    def statistics(j, done):
                        dve.wait_ge(y_done, done_at(done))
                        dve.wait_ge(std_done, free_at(done, 1))
                        dve.bn_stats(stat[:, :], p_y).then_inc(stat_done, 1)
                        dve.wait_ge(stat_done, done + 1)
                        hold(dve)
                        dve.bn_aggr(mean_var[:, :], stat[:, :]).then_inc(var_done, 1)

                    def scale(j, done):
                        dve.wait_ge(std_done, done_at(done))
                        dve.reciprocal(std[:, :], std[:, :]).then_inc(rstd_done, 1)
                        dve.wait_ge(row_free, free_at(done, 1))
                        dve.wait_ge(turned, free_at(done, 1))
                        dve.wait_ge(rstd_done, done + 1)
                        dve.tensor_tensor(row[:, :], p_y, std[:, :].broadcast_to([NB, D]), ALU.mult)\
                            .then_inc(row_done, 1)

                    def residual(j, done):
                        dve.wait_ge(std_done, done_at(done))
                        dve.reciprocal(std[:, :], std[:, :]).then_inc(rstd_done, 1)
                        dve.wait_ge(mid_free, free_at(done, 1))
                        dve.wait_ge(row_done, free_at(done, 1))
                        dve.wait_ge(x_ready, done * 16 + 16)
                        dve.wait_ge(rstd_done, done + 1)
                        hold(dve)
                        dve.scalar_tensor_tensor(out=mid[:, :], in0=p_y, scalar=std[:, 0:1],
                                                 in1=x_row[:, :], op0=ALU.mult, op1=ALU.add)\
                            .then_inc(mid_done, 1)
                        dve.wait_ge(std2_done, free_at(done, 1))
                        dve.wait_ge(mid_done, done_at(done))
                        dve.bn_stats(stat2[:, :], mid[:, :]).then_inc(stat2_done, 1)
                        dve.wait_ge(stat2_done, done + 1)
                        hold(dve)
                        dve.bn_aggr(mean_var2[:, :], stat2[:, :]).then_inc(var2_done, 1)

                    def normalise(j, done):
                        dve.wait_ge(std2_done, done_at(done))
                        dve.reciprocal(std2[:, :], std2[:, :]).then_inc(rstd2_done, 1)
                        dve.wait_ge(rstd2_done, done + 1)
                        dve.wait_ge(row_done, free_at(done, 1))
                        dve.scalar_tensor_tensor(out=shift[:, :], in0=mean_var2[:, 0:1], scalar=-1.0,
                                                 in1=std2[:, :], op0=ALU.mult, op1=ALU.mult)\
                            .then_inc(norm_done, 1)

                    chain = [(statistics, 13)] + ([(residual, 14), (normalise, 15)] if last else [(scale, 14)])
                    with dve.Fori(0, rounds) as r:
                        def hots(chunk, k, count, body):
                            dve.wait_ge(seg_done, free_at(count, BACK5[k]))
                            one_hot(dve, chunk, k).then_inc(hot_done, 1)

                        def add(chunk, k, count, body):
                            dve.wait_ge(seg_done, done_at(count))
                            dve.wait_ge(added, free_at(count, 1))
                            hold(dve)
                            add_window(dve, chunk, p_seg[:, k, 0:WIN], start_reg).then_inc(added, 1)

                        skewed(dve, BODIES, r * BODIES, [(hots, 0), (add, 1)], chain[::-1],
                               r * (BODIES - 1))
                        move_windows(dve, moved, r)
                    dve.wait_ge(added, rounds * CHUNKS + CREDIT)
                    hold(dve)
                    left_blocks(dve, [stage for stage, _ in chain])
                    restore_windows(dve, back)

        def gated_pass(name, table):
            with ExitStack() as own:
                names, slots = semaphores(own)

                def tmp(n, shape):
                    return own.enter_context(nc.sbuf_tensor(name + n, shape, F32))

                p_edge = own.enter_context(nc.psum_tensor(name + "edge", [P, 2, 3, 512], F32))
                p_seg = own.enter_context(nc.psum_tensor(name + "seg", [D1, 512], F32))
                p_node = own.enter_context(nc.psum_tensor(name + "node", [P, 512], F32))
                p_hidden, p_y = p_node[0:D, 0:NB], p_node[0:NB, 256:256 + D]
                hidden, h_block = tmp("hidden", [D, NB]), tmp("h_block", [D1, NB])
                stat, mean_var, std = tmp("stat", [NB, 6]), tmp("mv", [NB, 2]), tmp("std", [NB, 1])
                x_row, cent, row = tmp("x_row", [NB, D]), tmp("cent", [NB, D]), tmp("row", [NB, D])
                idx_ready, gathered = slots(name + "idx_ready"), slots(name + "gathered")
                edge_ready = slots(name + "edge_ready")
                (edge_done, pre_done, msg_done, gelu_done, z_done, tanh_done, gate_done, eq_done,
                 hot_done, seg_done, added, zeroed, moved, x_ready, up_done, h_copied, hidden_done,
                 y_done, stat_done, var_done, std_done, rstd_done, cent_done,
                 base_done, out_done, out_stored, out_free) = names(
                    *(name + n for n in (
                        "edge_done", "pre_done", "msg_done", "gelu_done", "z_done", "tanh_done",
                        "gate_done", "eq_done", "hot_done", "seg_done", "added", "zeroed", "moved",
                        "x_ready", "up_done", "h_copied", "hidden_done", "y_done",
                        "stat_done", "var_done", "std_done", "rstd_done", "cent_done", "base_done",
                        "out_done", "out_stored", "out_free")))
                block = own.enter_context(nc.Block())

                def halves(k):
                    return got[:, k, :].rearrange("p (t h f) -> p t h f", h=2, f=D)

                @block.sync
                def _(sp):
                    sp.sem_inc(out_free, CREDIT)
                    rounds = rounds_of(sp)

                    def attributes(chunk, k, count, body):
                        sp.wait_ge(edge_done, free_at(count, BACK5[k]))
                        sp.dma_start(edge[:, k, :], edge_t[:, bass.ds(chunk * CE, CE)])\
                            .then_inc(edge_ready[k], 16)

                    def load(j, done):
                        sp.wait_ge(out_done, free_at(done, 1))
                        sp.dma_start(x_row[:, :], block_rows(x_mid, j)).then_inc(x_ready, 16)

                    def store(j, done):
                        sp.wait_ge(out_done, done_at(done))
                        sp.dma_start(block_rows(out, j), row[:, :]).then_inc(out_stored, 16)

                    def is_stored(j, done):
                        sp.wait_ge(out_stored, done * 16 + 16)
                        sp.sem_inc(out_free, 1)

                    with sp.Fori(0, rounds) as r:
                        skewed(sp, BODIES, r * BODIES,
                               [(load_index(sp, idx_ready, pre_done), 0), (attributes, 0)],
                               [(load, 19), (store, 24), (is_stored, 25)], r * (BODIES - 1))
                    left_blocks(sp, [load, store, is_stored])

                @block.gpsimd
                def _(pool):
                    gather_rows(pool, table, 2 * D, 2 * D, idx_ready, gathered, z_done)

                @block.tensor
                def _(pe):
                    pe.sem_inc(seg_done, CREDIT)
                    pe.sem_inc(edge_done, CREDIT)
                    pe.sem_inc(y_done, CREDIT)
                    rounds = rounds_of(pe)
                    at_reg = pe.alloc_register(name + "at")

                    def up(j, done, at):
                        pe.wait_ge(hidden_done, free_at(done, 1))
                        pe.wait_ge(cent_done, free_at(done, 1))
                        hold(pe)
                        pe.matmul(p_hidden, wu_self[:, :], feat[:, bass.ds(at, NB)], start=True, stop=False)
                        pe.matmul(p_hidden, wu_sum[:, :], sums[0:D1, bass.ds(at, NB)], start=False,
                                  stop=True).then_inc(up_done, 1)

                    def down(j, done):
                        pe.wait_ge(h_copied, done + 1)
                        pe.wait_ge(hidden_done, done_at(done))
                        hold(pe)
                        pe.matmul(p_y, hidden[:, :], uw2[:, :], start=True, stop=False)
                        pe.matmul(p_y, h_block[:, :], ident_b[:, :], start=False, stop=True)\
                            .then_inc(y_done, 1)

                    with pe.Fori(0, rounds) as r:
                        def edges(chunk, k, count, body):
                            pe.wait_ge(edge_ready[k], body * 16 + 16)
                            pe.wait_ge(pre_done, free_at(count, BACK2[k]))
                            for t in range(TILES):
                                i = pe.matmul(p_edge[:, RING2[k], t // 2, t % 2 * 2 * D:(t % 2 + 1) * 2 * D],
                                              edge[:, k, t * P:(t + 1) * P], w_edge[:, :],
                                              start=True, stop=True)
                            i.then_inc(edge_done, 1)

                        def segment(chunk, k, count, body):
                            pe.wait_ge(msg_done, count + 1)
                            pe.wait_ge(hot_done, count + 1)
                            pe.wait_ge(added, free_at(count, 1))
                            for t in range(TILES):
                                i = pe.matmul(p_seg[:, 0:WIN], msg[:, k, t, :], hot[:, k, t, :],
                                              start=t == 0, stop=t == TILES - 1)
                            i.then_inc(seg_done, 1)

                        def up_within(j, done):
                            pe.wait_ge(added, (r * BODIES + j) * UNROLL + (2 * UNROLL + CREDIT))
                            hold(pe)
                            up(j, done, columns_at(pe, at_reg, j))

                        skewed(pe, BODIES, r * BODIES, [(edges, 0), (segment, 3)],
                               [(down, 16), (up_within, 14)], r * (BODIES - 1))
                    pe.wait_ge(added, rounds * CHUNKS + CREDIT)
                    hold(pe)
                    left_blocks(pe, [in_place(up), down])

                @block.scalar
                def _(act):
                    act.sem_inc(hidden_done, CREDIT)
                    act.sem_inc(std_done, CREDIT)
                    rounds = rounds_of(act)

                    at_reg = act.alloc_register(name + "act_at")

                    def gelu(j, done, at):
                        act.wait_ge(up_done, done + 1)
                        act.wait_ge(y_done, free_at(done, 1))
                        hold(act)
                        act.activation(h_block[:, :], feat[:, bass.ds(at, NB)], ACT.Copy)\
                            .then_inc(h_copied, 1)
                        act.activation(hidden[:, :], p_hidden, ACT.Gelu).then_inc(hidden_done, 1)

                    def gelu_within(j, done):
                        gelu(j, done, columns_at(act, at_reg, j))

                    def root(j, done):
                        act.wait_ge(var_done, done + 1)
                        act.wait_ge(out_done, free_at(done, 1))
                        act.activation(std[:, :], mean_var[:, 1:2], ACT.Sqrt, bias=eps_col[:, :])\
                            .then_inc(std_done, 1)

                    with act.Fori(0, rounds) as r:
                        def gelus(chunk, k, count, body):
                            act.wait_ge(pre_done, done_at(count))
                            act.activation(halves(k)[:, :, 1, :], halves(k)[:, :, 1, :], ACT.Gelu)\
                                .then_inc(gelu_done, 1)
                            act.wait_ge(seg_done, free_at(count, BACK5[k]))
                            act.activation(msg[:, k, :, 0:D], halves(k)[:, :, 0, :], ACT.Gelu)\
                                .then_inc(msg_done, 1)

                        def tanh(chunk, k, count, body):
                            act.wait_ge(z_done, done_at(count))
                            act.activation(gate[:, k, :], zz[:, k, :], ACT.Tanh, scale=0.5,
                                           bias=gb2_half[:, :]).then_inc(tanh_done, 1)

                        skewed(act, BODIES, r * BODIES, [(gelus, 0), (tanh, 1)],
                               [(root, 17), (gelu_within, 14)], r * (BODIES - 1))
                    left_blocks(act, [in_place(gelu), root])

                @block.vector
                def _(dve):
                    dve.sem_inc(pre_done, CREDIT)
                    dve.sem_inc(z_done, CREDIT)
                    dve.sem_inc(added, CREDIT)
                    dve.sem_inc(cent_done, CREDIT)
                    dve.sem_inc(out_done, CREDIT)
                    rounds = rounds_of(dve)
                    start_reg = dve.alloc_register(name + "start")
                    dve.memset(sums[:, :], 0.0).then_inc(zeroed, 1)
                    dve.wait_ge(zeroed, 1)
                    hold(dve)

                    def centre(j, done):
                        dve.wait_ge(y_done, done_at(done))
                        dve.wait_ge(std_done, free_at(done, 1))
                        dve.bn_stats(stat[:, :], p_y).then_inc(stat_done, 1)
                        dve.wait_ge(x_ready, done * 16 + 16)
                        dve.tensor_tensor(x_row[:, :], x_row[:, :], lnb_row[:, :], ALU.add)\
                            .then_inc(base_done, 1)
                        dve.wait_ge(stat_done, done + 1)
                        hold(dve)
                        dve.bn_aggr(mean_var[:, :], stat[:, :]).then_inc(var_done, 1)
                        dve.wait_ge(var_done, done + 1)
                        hold(dve)
                        dve.scalar_tensor_tensor(out=cent[:, :], in0=p_y, scalar=mean_var[:, 0:1],
                                                 in1=lng_row[:, :], op0=ALU.subtract, op1=ALU.mult)\
                            .then_inc(cent_done, 1)

                    def finish(j, done):
                        dve.wait_ge(std_done, done_at(done))
                        dve.reciprocal(std[:, :], std[:, :]).then_inc(rstd_done, 1)
                        dve.wait_ge(rstd_done, done + 1)
                        dve.wait_ge(cent_done, done_at(done))
                        dve.wait_ge(base_done, done + 1)
                        dve.wait_ge(out_free, free_at(done, 1))
                        hold(dve)
                        dve.scalar_tensor_tensor(out=row[:, :], in0=cent[:, :], scalar=std[:, 0:1],
                                                 in1=x_row[:, :], op0=ALU.mult, op1=ALU.add)\
                            .then_inc(out_done, 1)

                    with dve.Fori(0, rounds) as r:
                        def pre(chunk, k, count, body):
                            dve.wait_ge(gathered[k], gathered_at(body))
                            dve.wait_ge(edge_done, done_at(count))
                            four = got[:, k, 0:8 * D].rearrange("p (b f) -> p b f", b=2)
                            dve.tensor_tensor(four, four, p_edge[:, RING2[k], 0:2, 0:4 * D], ALU.add)
                            one = got[:, k, 8 * D:10 * D]
                            dve.tensor_tensor(one, one, p_edge[:, RING2[k], 2, 0:2 * D], ALU.add)\
                                .then_inc(pre_done, 1)

                        def gate_sums(chunk, k, count, body):
                            dve.wait_ge(gelu_done, count + 1)
                            dve.wait_ge(msg_done, count + 1)
                            for t in range(TILES):
                                half = halves(k)[:, t, 1, :]
                                i = dve.tensor_tensor_reduce(out=half, in0=half, in1=gw2_row[:, :],
                                                             scale=1.0, scalar=0.0, op0=ALU.mult,
                                                             op1=ALU.add, accum_out=zz[:, k, t:t + 1])
                            i.then_inc(z_done, 1)

                        def gated_hots(chunk, k, count, body):
                            dve.wait_ge(seg_done, free_at(count, BACK5[k]))
                            one_hot(dve, chunk, k).then_inc(eq_done, 1)
                            dve.wait_ge(tanh_done, count + 1)
                            dve.tensor_scalar(gate[:, k, :], gate[:, k, :], 0.5, 0.5, ALU.mult,
                                              ALU.add).then_inc(gate_done, 1)
                            dve.wait_ge(eq_done, count + 1)
                            dve.wait_ge(gate_done, count + 1)
                            dve.tensor_tensor(hot[:, k, :, :], hot[:, k, :, :],
                                              gate[:, k, :].unsqueeze(2).broadcast_to([P, TILES, WIN]),
                                              ALU.mult).then_inc(hot_done, 1)

                        def add(chunk, k, count, body):
                            dve.wait_ge(seg_done, done_at(count))
                            dve.wait_ge(added, free_at(count, 1))
                            hold(dve)
                            add_window(dve, chunk, p_seg[:, 0:WIN], start_reg).then_inc(added, 1)

                        skewed(dve, BODIES, r * BODIES,
                               [(pre, 0), (gate_sums, 1), (gated_hots, 2), (add, 3)],
                               [(finish, 18), (centre, 16)], r * (BODIES - 1))
                        move_windows(dve, moved, r)
                    dve.wait_ge(added, rounds * CHUNKS + CREDIT)
                    hold(dve)
                    left_blocks(dve, [centre, finish])

        node_norm_first()
        linear_pass("l0_", 0, rows_h, False)
        linear_pass("l1_", 1, rows_x1, True)
        gated_pass("g_", rows_p)


def kernel(**inputs):
    import numpy as np
    import concourse.bacc as bacc
    from concourse.bass_utils import run_bass_kernel_spmd

    a = {name: np.asarray(value) for name, value in inputs.items()}
    g = {name[len("L1_gnn_"):]: value for name, value in a.items() if name.startswith("L1_gnn_")}
    l = {name[len("L0_gnn_"):]: value for name, value in a.items() if name.startswith("L0_gnn_")}
    laid = {
        "x": a["x"],
        "src": a["src"].reshape(CHUNKS, TILES, P).transpose(0, 2, 1),
        "dst_tiles": a["dst"].reshape(CHUNKS * TILES, P).T,
        "dst_rows": a["dst"].reshape(BODIES, UNROLL, CE),
        "edge_t": a["edge_attr_32"].T,
        "W0T": l["W0"].transpose(0, 2, 1), "b0": l["b0"].reshape(2, D, 1),
        "W1T": l["W1"].transpose(0, 2, 1), "b1": l["b1"].reshape(2, D, 1),
        "W2": l["W2"], "b2": l["b2"].reshape(2, 1, D),
        "mW1": g["mW1"], "mb1": g["mb1"].reshape(1, D), "mW2T": g["mW2"].T, "mb2": g["mb2"].reshape(D, 1),
        "gW1": g["gW1"], "gb1": g["gb1"].reshape(1, D), "gW2": g["gW2"].reshape(D), "gb2": g["gb2"],
        "uW1": g["uW1"], "ub1": g["ub1"].reshape(1, D), "uW2": g["uW2"], "ub2": g["ub2"].reshape(1, D),
        "ln_g": g["ln_g"], "ln_b": g["ln_b"],
    }
    nc = bacc.Bacc("TRN2", target_bir_lowering=False, num_devices=1)
    arrays, args = {}, []
    for name, value in laid.items():
        value = np.ascontiguousarray(value)
        arrays[f"in_{name}"] = value
        args.append(nc.dram_tensor(f"in_{name}", value.shape, mybir.dt.from_np(value.dtype),
                                   kind="ExternalInput").ap())
    args.append(nc.dram_tensor("out", (N, D), F32, kind="ExternalOutput").ap())
    for name, shape in (("rows_h", (N, D)), ("rows_x1", (N, D)), ("rows_p", (N, 2 * D)),
                        ("x_mid", (N, D)), ("extents", (2, BODIES, UNROLL))):
        args.append(nc.dram_tensor(name, shape, F32, kind="Internal").ap())
    gnn(nc, *args)
    r = run_bass_kernel_spmd(nc, [arrays], core_ids=[0])
    return r.results[0]["out"]
```
